# Optimizing a Trainium2 kernel written in Bass

```python
import numpy as np
import jax
import jax.numpy as jnp

def _softmax(x, axis=-1):
    return jax.nn.softmax(x, axis=axis)

def _gelu(x):
    return jax.nn.gelu(x, approximate=True)

def _silu(x):
    return jax.nn.silu(x)

def _sigmoid(x):
    return jax.nn.sigmoid(x)

def _layernorm(x, axis=-1, eps=1e-05):
    m = jnp.mean(x, axis=axis, keepdims=True)
    v = jnp.var(x, axis=axis, keepdims=True)
    return (x - m) / jnp.sqrt(v + eps)

def _scatter_add(tgt, idx, src, axis=0):
    return tgt.at[idx].add(src)

def _segment_sum(src, seg, n):
    return jax.ops.segment_sum(src, seg, n)
kernel_name = 'mk_gnn_preln_d4_gnn_r32_cabd5a'

def setup_inputs(seed: int=0):
    np.random.seed(seed)
    _w = jnp.asarray

    def _rec_inputs():
        import jax
        import jax.numpy as jnp
        _gk = jax.random.key(seed)
        x = -0.0004942 + 1 * jax.random.normal(jax.random.fold_in(_gk, 1), (3125, 128), jnp.float32)
        src = jax.random.randint(jax.random.fold_in(_gk, 2), (100000,), 0, 3125, jnp.int32)
        dst = jax.random.randint(jax.random.fold_in(_gk, 3), (100000,), 0, 3125, jnp.int32)
        _o = jnp.argsort(dst, stable=True)
        src = src[_o]
        dst = dst[_o]
        edge_type_32 = jax.random.randint(jax.random.fold_in(_gk, 13), (100000,), 0, 32, jnp.int32)
        edge_weight1 = jax.random.uniform(jax.random.fold_in(_gk, 14), (100000, 1), jnp.float32, 0.0, 0.999998)
        return (x, src, dst, edge_type_32, edge_weight1)
    x, src, dst, edge_type_32, edge_weight1 = _rec_inputs()

    def _L0_gnn_setup():
        import jax, jax.numpy as jnp
        import numpy as np
        N = 30000
        E = 30000
        DIN = 128
        DOUT = 128
        R = 32
        NUM_RULES = 100
        ACTIVE = 4
        EPS = 1e-05
        key = jax.random.key(seed)
        ks = jax.random.split(key, 10)
        x = jax.random.normal(ks[0], (N, DIN), jnp.float32)
        src = jax.random.randint(ks[1], (E,), 0, N)
        dst = jax.random.randint(ks[2], (E,), 0, N)
        edge_type = jax.random.randint(ks[3], (E,), 0, R)
        rule_ids = jax.random.randint(ks[4], (ACTIVE,), 0, NUM_RULES)
        W_r = jax.random.normal(ks[5], (R, DIN, DOUT), jnp.float32) * 0.05
        Wq_w = jax.random.normal(ks[6], (DIN, DOUT), jnp.float32) * 0.05
        Wq_b = jnp.zeros((DOUT,), jnp.float32)
        Wk_w = jax.random.normal(ks[7], (3 * DIN, DOUT), jnp.float32) * 0.05
        Wk_b = jnp.zeros((DOUT,), jnp.float32)
        rule_emb = jax.random.normal(ks[8], (NUM_RULES, DIN), jnp.float32) * 0.05
        bias = jnp.zeros((DOUT,), jnp.float32)
        ln_gamma = jnp.ones((DOUT,), jnp.float32)
        ln_beta = jnp.zeros((DOUT,), jnp.float32)
        return {'x': x, 'W_r': W_r, 'Wq_w': Wq_w, 'Wq_b': Wq_b, 'Wk_w': Wk_w, 'Wk_b': Wk_b, 'rule_emb': rule_emb, 'bias': bias, 'ln_gamma': ln_gamma, 'ln_beta': ln_beta, 'src': src, 'dst': dst, 'edge_type': edge_type, 'rule_ids': rule_ids}
    _L0_gnn_all = _L0_gnn_setup()
    _L0_gnn_in = {k: v for k, v in _L0_gnn_all.items() if k in ('W_r', 'Wq_w', 'Wq_b', 'Wk_w', 'Wk_b', 'rule_emb', 'bias', 'ln_gamma', 'ln_beta', 'rule_ids')}
    del _L0_gnn_all

    def _L1_gnn_setup():
        import jax, jax.numpy as jnp
        import numpy as np
        key = jax.random.key(seed)
        k1, k2, k3 = jax.random.split(key, 3)
        N, E, D = (50000, 18750, 128)
        x = jax.random.normal(k1, (N, D), dtype=jnp.float32)
        src = jax.random.randint(k2, (E,), 0, N, dtype=jnp.int64)
        dst = jax.random.randint(k3, (E,), 0, N, dtype=jnp.int64)
        return {'x': x, 'src': src, 'dst': dst}
    _L1_gnn_all = _L1_gnn_setup()
    _L1_gnn_in = {k: v for k, v in _L1_gnn_all.items() if k in ()}
    del _L1_gnn_all

    def _L2_gnn_setup():
        import jax, jax.numpy as jnp
        import numpy as np
        NUM_NODES = 3125
        NUM_EDGES = 20000
        D_FEAT = 128
        key = jax.random.key(seed)
        k1, k2 = jax.random.split(key)
        embeddings = jax.random.normal(k1, (NUM_NODES, D_FEAT), dtype=jnp.float32)
        edge_index = jax.random.randint(k2, (2, NUM_EDGES), 0, NUM_NODES, dtype=jnp.int64)
        return {'embeddings': embeddings, 'edge_index': edge_index}
    _L2_gnn_all = _L2_gnn_setup()
    _L2_gnn_in = {k: v for k, v in _L2_gnn_all.items() if k in ()}
    del _L2_gnn_all

    def _L3_gnn_setup():
        import jax, jax.numpy as jnp
        import numpy as np
        N, E, IN_DIM, HID, HEADS, LAYERS = (50000, 10000, 128, 128, 4, 2)
        C = HID // HEADS
        EPS = 1e-05

        def _init(key, shape, fan_in):
            return jax.random.normal(key, shape, dtype=jnp.float32) / np.sqrt(fan_in)

        def _transformer_conv(h, src, tgt, edge_attr, Wq, bq, Wk, bk, Wv, bv, We, Wskip, bskip, Wbeta):
            n = h.shape[0]
            q = (h @ Wq + bq).reshape(n, HEADS, C)
            k = (h @ Wk + bk).reshape(n, HEADS, C)
            v = (h @ Wv + bv).reshape(n, HEADS, C)
            e = (edge_attr @ We).reshape(-1, HEADS, C)
            k_j = k[src] + e
            alpha = jnp.einsum('ehc,ehc->eh', q[tgt], k_j) / jnp.sqrt(jnp.float32(C))
            amax = jax.ops.segment_max(alpha, tgt, num_segments=n)
            ex = jnp.exp(alpha - amax[tgt])
            denom = jax.ops.segment_sum(ex, tgt, num_segments=n)
            a = ex / denom[tgt]
            msg = (v[src] + e) * a[..., None]
            out = jax.ops.segment_sum(msg, tgt, num_segments=n).reshape(n, HID)
            x_r = h @ Wskip + bskip
            beta = jax.nn.sigmoid(jnp.concatenate([out, x_r, out - x_r], axis=-1) @ Wbeta)
            return beta * x_r + (1.0 - beta) * out

        def _batchnorm(h, gamma, beta):
            mu = h.mean(axis=0)
            var = h.var(axis=0)
            return gamma * (h - mu) * jax.lax.rsqrt(var + EPS) + beta
        key = jax.random.key(seed)
        ks = jax.random.split(key, 20)
        x = jax.random.normal(ks[0], (N, IN_DIM), dtype=jnp.float32)
        edge_index = jax.random.randint(ks[1], (2, E), 0, N, dtype=jnp.int64)
        edge_attr = jax.random.uniform(ks[2], (E, 1), dtype=jnp.float32)
        inp = {'x': x, 'edge_index': edge_index, 'edge_attr': edge_attr, 'W_in': _init(ks[3], (IN_DIM, HID), IN_DIM), 'b_in': jnp.zeros((HID,), jnp.float32), 'Wq': _init(ks[4], (LAYERS, HID, HID), HID), 'bq': jnp.zeros((LAYERS, HID), jnp.float32), 'Wk': _init(ks[5], (LAYERS, HID, HID), HID), 'bk': jnp.zeros((LAYERS, HID), jnp.float32), 'Wv': _init(ks[6], (LAYERS, HID, HID), HID), 'bv': jnp.zeros((LAYERS, HID), jnp.float32), 'We': _init(ks[7], (LAYERS, 1, HID), 1), 'Wskip': _init(ks[8], (LAYERS, HID, HID), HID), 'bskip': jnp.zeros((LAYERS, HID), jnp.float32), 'Wbeta': _init(ks[9], (LAYERS, 3 * HID, 1), 3 * HID), 'bn_gamma': jnp.ones((LAYERS, HID), jnp.float32), 'bn_beta': jnp.zeros((LAYERS, HID), jnp.float32)}
        return inp
    _L3_gnn_all = _L3_gnn_setup()
    _L3_gnn_in = {k: v for k, v in _L3_gnn_all.items() if k in ('W_in', 'b_in', 'Wq', 'bq', 'Wk', 'bk', 'Wv', 'bv', 'We', 'Wskip', 'bskip', 'Wbeta', 'bn_gamma', 'bn_beta')}
    del _L3_gnn_all
    return {'x': x, 'src': src, 'dst': dst, 'edge_type_32': edge_type_32, 'edge_weight1': edge_weight1, 'L0_gnn_W_r': _L0_gnn_in['W_r'], 'L0_gnn_Wq_w': _L0_gnn_in['Wq_w'], 'L0_gnn_Wq_b': _L0_gnn_in['Wq_b'], 'L0_gnn_Wk_w': _L0_gnn_in['Wk_w'], 'L0_gnn_Wk_b': _L0_gnn_in['Wk_b'], 'L0_gnn_rule_emb': _L0_gnn_in['rule_emb'], 'L0_gnn_bias': _L0_gnn_in['bias'], 'L0_gnn_ln_gamma': _L0_gnn_in['ln_gamma'], 'L0_gnn_ln_beta': _L0_gnn_in['ln_beta'], 'L0_gnn_rule_ids': _L0_gnn_in['rule_ids'], 'L3_gnn_W_in': _L3_gnn_in['W_in'], 'L3_gnn_b_in': _L3_gnn_in['b_in'], 'L3_gnn_Wq': _L3_gnn_in['Wq'], 'L3_gnn_bq': _L3_gnn_in['bq'], 'L3_gnn_Wk': _L3_gnn_in['Wk'], 'L3_gnn_bk': _L3_gnn_in['bk'], 'L3_gnn_Wv': _L3_gnn_in['Wv'], 'L3_gnn_bv': _L3_gnn_in['bv'], 'L3_gnn_We': _L3_gnn_in['We'], 'L3_gnn_Wskip': _L3_gnn_in['Wskip'], 'L3_gnn_bskip': _L3_gnn_in['bskip'], 'L3_gnn_Wbeta': _L3_gnn_in['Wbeta'], 'L3_gnn_bn_gamma': _L3_gnn_in['bn_gamma'], 'L3_gnn_bn_beta': _L3_gnn_in['bn_beta']}

def reference(x, src, dst, edge_type_32, edge_weight1, L0_gnn_W_r, L0_gnn_Wq_w, L0_gnn_Wq_b, L0_gnn_Wk_w, L0_gnn_Wk_b, L0_gnn_rule_emb, L0_gnn_bias, L0_gnn_ln_gamma, L0_gnn_ln_beta, L0_gnn_rule_ids, L3_gnn_W_in, L3_gnn_b_in, L3_gnn_Wq, L3_gnn_bq, L3_gnn_Wk, L3_gnn_bk, L3_gnn_Wv, L3_gnn_bv, L3_gnn_We, L3_gnn_Wskip, L3_gnn_bskip, L3_gnn_Wbeta, L3_gnn_bn_gamma, L3_gnn_bn_beta):
    import jax
    import jax.numpy as jnp

    def _L0_gnn_ref(x, W_r, Wq_w, Wq_b, Wk_w, Wk_b, rule_emb, bias, ln_gamma, ln_beta, src, dst, edge_type, rule_ids):
        import jax, jax.numpy as jnp
        import numpy as np
        N = 30000
        E = 30000
        DIN = 128
        DOUT = 128
        R = 32
        NUM_RULES = 100
        ACTIVE = 4
        EPS = 1e-05
        n_nodes, _ = x.shape
        n_rel, _, dout = W_r.shape
        scale = 1.0 / jnp.sqrt(jnp.float32(dout))
        h_R = rule_emb[rule_ids]
        q = (x @ Wq_w + Wq_b)[dst]
        Wk1, Wk2, Wk3 = jnp.split(Wk_w, 3, axis=0)
        h_rel = W_r.mean(axis=-1)
        k_node = x @ Wk1
        k_rel = h_rel @ Wk2
        v_rule = h_R @ Wk3
        k_base = k_node[src] + k_rel[edge_type] + Wk_b
        score_base = jnp.sum(q * k_base, axis=-1)
        scores = (score_base[:, None] + q @ v_rule.T) * scale
        seg = edge_type * n_nodes + dst
        nseg = n_rel * n_nodes
        m = jax.ops.segment_max(scores, seg, num_segments=nseg)
        ex = jnp.exp(scores - m[seg])
        s = jax.ops.segment_sum(ex, seg, num_segments=nseg)
        attn = ex / s[seg]
        attn_mean = attn.mean(axis=-1)
        proj = jnp.einsum('nd,rdo->nro', x, W_r)
        msg = proj[src, edge_type] * attn_mean[:, None]
        out = jax.ops.segment_sum(msg, dst, num_segments=n_nodes) + bias
        mu = out.mean(axis=-1, keepdims=True)
        var = out.var(axis=-1, keepdims=True)
        out = (out - mu) * jax.lax.rsqrt(var + EPS) * ln_gamma + ln_beta
        return jax.nn.relu(out)

    def _L1_gnn_ref(x, src, dst):
        import jax, jax.numpy as jnp
        import numpy as np
        N = x.shape[0]
        loop = jnp.arange(N, dtype=src.dtype)
        s = jnp.concatenate([src, loop])
        d = jnp.concatenate([dst, loop])
        ones = jnp.ones(s.shape[0], dtype=x.dtype)
        in_deg = jax.ops.segment_sum(ones, d, num_segments=N)
        out_deg = jax.ops.segment_sum(ones, s, num_segments=N)
        norm_in = jnp.clip(in_deg, 1.0) ** (-0.5)
        norm_out = jnp.clip(out_deg, 1.0) ** (-0.5)
        xs = x * norm_in[:, None]
        h = jax.ops.segment_sum(xs[s], d, num_segments=N)
        return h * norm_out[:, None]

    def _L2_gnn_ref(embeddings, edge_index):
        import jax, jax.numpy as jnp
        import numpy as np
        NUM_NODES = 3125
        NUM_EDGES = 20000
        D_FEAT = 128
        'LightGCN propagation: out[v] = sum_{(u,v) in E} e[u] / (sqrt(deg(u)) * sqrt(deg(v)))\n            where deg is the out-degree computed from the row (source) indices.'
        num_nodes = embeddings.shape[0]
        row, col = (edge_index[0], edge_index[1])
        deg = jax.ops.segment_sum(jnp.ones_like(row, dtype=embeddings.dtype), row, num_segments=num_nodes)
        deg = jnp.maximum(deg, 1.0)
        deg_inv_sqrt = deg ** (-0.5)
        norm = deg_inv_sqrt[row] * deg_inv_sqrt[col]
        msgs = embeddings[row] * norm[:, None]
        out = jax.ops.segment_sum(msgs, col, num_segments=num_nodes)
        return out

    def _L3_gnn_ref(x, edge_index, edge_attr, W_in, b_in, Wq, bq, Wk, bk, Wv, bv, We, Wskip, bskip, Wbeta, bn_gamma, bn_beta):
        import jax, jax.numpy as jnp
        import numpy as np
        N, E, IN_DIM, HID, HEADS, LAYERS = (50000, 10000, 128, 128, 4, 2)
        C = HID // HEADS
        EPS = 1e-05

        def _init(key, shape, fan_in):
            return jax.random.normal(key, shape, dtype=jnp.float32) / np.sqrt(fan_in)

        def _transformer_conv(h, src, tgt, edge_attr, Wq, bq, Wk, bk, Wv, bv, We, Wskip, bskip, Wbeta):
            n = h.shape[0]
            q = (h @ Wq + bq).reshape(n, HEADS, C)
            k = (h @ Wk + bk).reshape(n, HEADS, C)
            v = (h @ Wv + bv).reshape(n, HEADS, C)
            e = (edge_attr @ We).reshape(-1, HEADS, C)
            k_j = k[src] + e
            alpha = jnp.einsum('ehc,ehc->eh', q[tgt], k_j) / jnp.sqrt(jnp.float32(C))
            amax = jax.ops.segment_max(alpha, tgt, num_segments=n)
            ex = jnp.exp(alpha - amax[tgt])
            denom = jax.ops.segment_sum(ex, tgt, num_segments=n)
            a = ex / denom[tgt]
            msg = (v[src] + e) * a[..., None]
            out = jax.ops.segment_sum(msg, tgt, num_segments=n).reshape(n, HID)
            x_r = h @ Wskip + bskip
            beta = jax.nn.sigmoid(jnp.concatenate([out, x_r, out - x_r], axis=-1) @ Wbeta)
            return beta * x_r + (1.0 - beta) * out

        def _batchnorm(h, gamma, beta):
            mu = h.mean(axis=0)
            var = h.var(axis=0)
            return gamma * (h - mu) * jax.lax.rsqrt(var + EPS) + beta
        src, tgt = (edge_index[0], edge_index[1])
        h = jax.nn.relu(x @ W_in + b_in)
        for l in range(LAYERS):
            h_res = h
            h = _transformer_conv(h, src, tgt, edge_attr, Wq[l], bq[l], Wk[l], bk[l], Wv[l], bv[l], We[l], Wskip[l], bskip[l], Wbeta[l])
            h = jax.nn.relu(_batchnorm(h, bn_gamma[l], bn_beta[l]))
            h = h + h_res
        return h
    edge_index = jnp.stack([src, dst])
    h = jnp.maximum(_layernorm(x, axis=-1), 0.0)
    x = x + _L0_gnn_ref(h, L0_gnn_W_r, L0_gnn_Wq_w, L0_gnn_Wq_b, L0_gnn_Wk_w, L0_gnn_Wk_b, L0_gnn_rule_emb, L0_gnn_bias, L0_gnn_ln_gamma, L0_gnn_ln_beta, src, dst, edge_type_32, L0_gnn_rule_ids)
    h = jnp.maximum(_layernorm(x, axis=-1), 0.0)
    x = x + _L1_gnn_ref(h, src, dst)
    h = jnp.maximum(_layernorm(x, axis=-1), 0.0)
    x = x + _L2_gnn_ref(h, edge_index)
    h = jnp.maximum(_layernorm(x, axis=-1), 0.0)
    x = x + _L3_gnn_ref(h, edge_index, edge_weight1, L3_gnn_W_in, L3_gnn_b_in, L3_gnn_Wq, L3_gnn_bq, L3_gnn_Wk, L3_gnn_bk, L3_gnn_Wv, L3_gnn_bv, L3_gnn_We, L3_gnn_Wskip, L3_gnn_bskip, L3_gnn_Wbeta, L3_gnn_bn_gamma, L3_gnn_bn_beta)
    return x

_drawn_inputs = setup_inputs


def setup_inputs(seed=0):
    import zlib

    import numpy as np

    out = dict(_drawn_inputs(seed))
    spreads = {'L0_gnn_Wq_b': (0.0, 0.8),
     'L0_gnn_Wk_b': (0.0, 0.8),
     'L0_gnn_bias': (0.0, 0.1),
     'L0_gnn_ln_gamma': (1.0, 0.2),
     'L0_gnn_ln_beta': (0.0, 0.1),
     'L3_gnn_b_in': (0.0, 0.1),
     'L3_gnn_bq': (0.0, 0.8),
     'L3_gnn_bk': (0.0, 0.8),
     'L3_gnn_bv': (0.0, 0.419),
     'L3_gnn_bskip': (0.0, 0.338),
     'L3_gnn_bn_gamma': (1.0, 0.2),
     'L3_gnn_bn_beta': (0.0, 0.1)}
    factors = {'L0_gnn_Wq_w': 3.181, 'L0_gnn_Wk_w': 3.073, 'L0_gnn_rule_emb': 8.0}
    for name, (base, spread) in spreads.items():
        noise = np.random.default_rng([zlib.crc32(name.encode()), seed]).standard_normal(out[name].shape)
        drawn = base * np.exp(spread * noise) if base else spread * noise
        out[name] = jnp.asarray(drawn.astype(out[name].dtype))
    for name, factor in factors.items():
        out[name] = (out[name] * factor).astype(out[name].dtype)
    return out
```

```python
from contextlib import ExitStack

import concourse.bass as bass
from concourse import mybir

F32 = mybir.dt.float32
I32 = mybir.dt.int32
ALU = mybir.AluOpType
ACT = mybir.ActivationFunctionType
AX = mybir.AxisListType.X

P = 128
D = 128
BIG = 1e30
EPS = 1e-5
GS = 4
NG = 4
IT = GS * NG
AHEAD = 2 * GS
W_ACC = 136


def ceil_div(a, b):
    return -(-a // b)


class Progress:
    DEPTH = 4

    def __init__(self, sem, actions):
        self.sem, self.actions, self.turn = sem.sem, list(actions), 0

    def credit(self, eng):
        eng.sem_inc(self.sem, self.DEPTH * len(self.actions))

    def at(self, group, action):
        k = len(self.actions)
        return (group + (self.DEPTH - 1)) * k + (self.actions.index(action) + 1)

    def did(self, action):
        assert self.actions[self.turn % len(self.actions)] == action, (action, self.turn)
        self.turn += 1
        return self.sem, 1


class Chain:

    def __init__(self, sem):
        self.sem, self.n = sem, 0

    def on(self, eng):
        def link(ins):
            self.n += 1
            ins.then_inc(self.sem, 1)
            eng.wait_ge(self.sem, self.n)
        return link


class Signal:

    def __init__(self, sem):
        self.sem, self.base = sem, 0

    def after(self, n):
        return self.base + n

    def passed(self, n):
        self.base += n


class Net:

    def __init__(self, nc, ctx, N, E, R):
        self.nc, self.ctx = nc, ctx
        self.N, self.E, self.R = N, E, R
        self.NT = ceil_div(N, P)
        self.NP = self.NT * P
        self.LAST = N - (self.NT - 1) * P
        self.C = ceil_div(E, P)
        self.ITERS = ceil_div(self.C + self.NT - 1, IT)
        self.S = self.ITERS * IT
        self.GROUPS = self.S // GS
        self.RG = ceil_div(self.S, P)
        self.V = self.S * P
        sem = lambda name: ctx.enter_context(nc.semaphore(name))
        self.dve = Chain(sem("dve_chain"))
        self.act = Chain(sem("act_chain"))
        self.pool = Chain(sem("pool_chain"))
        self.pe_done = Signal(sem("pe_done"))
        self.dve_done = Signal(sem("dve_done"))
        self.act_done = Signal(sem("act_done"))
        self.dve_rounds = Signal(sem("dve_rounds"))
        self.pool_done = Signal(sem("pool_done"))
        self.loaded = Signal(sem("loaded"))
        self.picked = Signal(sem("rows_picked"))
        self.stored = Signal(sem("stored"))
        self.weights_sem = sem("weights_loaded")
        self.pool_turn, self.act_turn, self.dve_turn = sem("pool_turn"), sem("act_turn"), sem("dve_turn")
        self.loops = 0
        self.used = {}

    def loop_sem(self, name):
        return Signal(self.ctx.enter_context(self.nc.semaphore(f"loop{self.loops}_{name}")))

    def gather_sems(self):
        self.loops += 1
        self.staged = self.loop_sem("indices_staged")
        return [self.loop_sem(f"gathered{g}") for g in range(NG)]

    def once(self, name):
        self.used[name] = self.used.get(name, 0) + 1
        return name if self.used[name] == 1 else f"{name}_{self.used[name]}"

    def sb(self, scope, name, shape, dt=F32):
        return scope.enter_context(self.nc.sbuf_tensor(self.once(name), shape, dt))

    def ps(self, scope, name, shape, dt=F32):
        return scope.enter_context(self.nc.psum_tensor(self.once(name), shape, dt))

    def sem(self, scope, name):
        return scope.enter_context(self.nc.semaphore(name))

    def dram(self, name, shape, dt=F32):
        return self.nc.dram_tensor(name, shape, dt).ap()


def wide(ap, at, n):
    u = ap.unsqueeze(at)
    shape = list(u.shape)
    shape[at] = n
    return u.to_broadcast(shape)



def load_edges(net, src, dst, typ, weight, x):
    nc, C, E = net.nc, net.C, net.E
    FULL = E // P
    G = FULL // P
    RF = FULL - G * P
    REST = E - FULL * P
    RG = net.RG
    CR = net.CR
    pad = net.NP - 1
    fields = [(src, 0), (dst, 1), (typ, 2), (weight, 3)]
    with nc.Block() as block:
        @block.vector
        def _(dve):
            dve.memset(net.X[:, net.NT - 1, :], 0.0)
            dve.memset(CR[:, :, 0, :], 0)
            dve.memset(CR[:, :, 2:4, :], 0)
            dve.memset(CR[:, :, 1, :], pad)
            dve.memset(CR[:, :, 4, :], pad).then_inc(net.dve_done.sem, 1)
            dve.memset(net.ones[:, :], 1.0)
            dve.memset(net.zero[:, :], 0.0)
            dve.memset(net.ident[:, :], 0.0).then_inc(net.dve_done.sem, 1)

        @block.sync
        def _(sp):
            n = 0

            def load(to, of):
                nonlocal n
                sp.dma_start(to, of).then_inc(net.loaded.sem, 16)
                n += 16

            sp.dma_start(net.X[:, 0:net.NT - 1, :], x[0:(net.NT - 1) * P, :].rearrange(
                "(t p) d -> p t d", p=P)).then_inc(net.loaded.sem, 16)
            n += 16
            sp.wait_ge(net.dve_done.sem, net.dve_done.after(1))
            load(net.X[0:net.LAST, net.NT - 1, :], x[(net.NT - 1) * P:net.N, :])
            for a, f in fields:
                load(CR[:, 0:G, f, :], a[0:G * P * P].rearrange("(g p q) -> p g q", p=P, q=P))
                load(CR[0:RF, G, f, :], a[G * P * P:FULL * P].rearrange("(p q) -> p q", q=P))
                if REST:
                    load(CR[RF:RF + 1, G, f, 0:REST], a[FULL * P:E].rearrange("(p q) -> p q", p=1))
            load(CR[0:1, 0, 4, 1:P], dst[0:P - 1].rearrange("(p q) -> p q", p=1))
            load(CR[1:P, 0, 4, :], dst[P - 1:P * P - 1].rearrange("(p q) -> p q", q=P))
            load(CR[:, 1:G, 4, :], dst[P * P - 1:G * P * P - 1].rearrange("(g p q) -> p g q", p=P, q=P))
            load(CR[0:RF, G, 4, :], dst[G * P * P - 1:FULL * P - 1].rearrange("(p q) -> p q", q=P))
            load(CR[RF:RF + 1, G, 4, 0:REST + 1], dst[FULL * P - 1:E].rearrange("(p q) -> p q", p=1))
            sp.wait_ge(net.loaded.sem, net.loaded.after(n))
            sp.dma_start(net.chunks.rearrange("(g p) f -> p g f", p=P),
                         CR[:, :, :, :].rearrange("p g f q -> p g (f q)")).then_inc(net.stored.sem, 16)
            sp.wait_ge(net.stored.sem, net.stored.after(16))
            net.loaded.passed(n)
            net.stored.passed(16)

        @block.gpsimd
        def _(pool):
            link = net.pool.on(pool)
            pool.wait_ge(net.dve_done.sem, net.dve_done.after(2))
            link(pool.affine_select(out=net.ident[:, :], in_=net.ident[:, :], compare_op=ALU.not_equal,
                                    fill=1.0, base=0, pattern=[[-1, P]], channel_multiplier=1))
            link(pool.iota(net.iota_i[:, :], pattern=[[1, P]], base=0, channel_multiplier=0))
            link(pool.tensor_copy(net.iota[:, :], net.iota_i[:, :]))
            link(pool.iota(net.step_i[:, :], pattern=[[P, RG]], base=0, channel_multiplier=1))
            link(pool.tensor_copy(net.step_f[:, :], net.step_i[:, :]))
    net.dve_done.passed(2)


def pair_steps(net):
    nc, RG, CR = net.nc, net.RG, net.CR
    KW = RG * P
    with ExitStack() as sc:
        last = net.sb(sc, "last_tile", [P, RG], I32)
        key = net.sb(sc, "chunk_key", [P, RG])
        keyw = net.sb(sc, "chunk_key_wide", [P, RG, P])
        keys = net.sb(sc, "keys_everywhere", [P, KW])
        below = net.sb(sc, "below", [P, KW])
        chunk_f = net.sb(sc, "chunk_f", [P, RG])
        tile_f = net.sb(sc, "tile_f", [P, RG])
        tile_w = net.sb(sc, "tile_w", [RG, P], I32)
        pk = net.ps(sc, "pk", [P, 2, 512])
        pt = net.ps(sc, "pt", [P, 512])
        with nc.Block() as block:
            @block.vector
            def _(dve):
                link = net.dve.on(dve)
                link(dve.tensor_scalar(last[:, :], CR[:, :, 1, P - 1], 7, None, ALU.logical_shift_right))
                link(dve.tensor_copy(key[:, :], last[:, :]))
                link(dve.tensor_tensor(key[:, :], key[:, :], net.step_f[:, :], ALU.add))
                dve.tensor_copy(keyw[:, :, :], wide(key[:, :], 2, P)).then_inc(net.dve_done.sem, 1)
                dve.wait_ge(net.pe_done.sem, net.pe_done.after(RG))
                link(dve.tensor_copy(keys[:, 0:512], pk[:, 0, :]))
                link(dve.tensor_copy(keys[:, 512:KW], pk[:, 1, 0:KW - 512]))
                for g in range(RG):
                    link(dve.tensor_tensor(below[:, :], keys[:, :],
                                           net.step_f[:, g:g + 1].to_broadcast([P, KW]), ALU.is_lt))
                    link(dve.tensor_reduce(chunk_f[:, g:g + 1], below[:, :], AX, ALU.add))
                link(dve.tensor_copy(net.chunk_i[:, :], chunk_f[:, :]))
                dve.tensor_tensor(tile_f[:, :], net.step_f[:, :], chunk_f[:, :],
                                  ALU.subtract).then_inc(net.dve_done.sem, 1)
                dve.wait_ge(net.dve_done.sem, net.dve_done.after(2))
                link(dve.tensor_scalar(tile_f[:, :], tile_f[:, :], float(net.NT - 1), None, ALU.min))
                dve.tensor_scalar(net.base128[:, :], tile_f[:, :], float(P), None,
                                  ALU.mult).then_inc(net.dve_done.sem, 1)
                dve.wait_ge(net.pe_done.sem, net.pe_done.after(RG + 1))
                dve.tensor_copy(tile_w[:, :], pt[0:RG, 0:P]).then_inc(net.dve_done.sem, 1)

            @block.tensor
            def _(pe):
                pe.wait_ge(net.dve_done.sem, net.dve_done.after(1))
                for g in range(RG):
                    pe.matmul(pk[:, g // 4, (g % 4) * P:(g % 4 + 1) * P], keyw[:, g, :], net.ident[:, :],
                              start=True, stop=True).then_inc(net.pe_done.sem, 1)
                pe.wait_ge(net.dve_done.sem, net.dve_done.after(3))
                pe.transpose(pt[0:RG, 0:P], tile_f[:, :], net.ident[:, :]).then_inc(net.pe_done.sem, 1)

            @block.gpsimd
            def _(pool):
                pool.wait_ge(net.dve_done.sem, net.dve_done.after(2))
                for g in range(RG):
                    pool.indirect_dma_start(
                        out=net.VR[:, g, :, :].rearrange("p f q -> p (f q)"), out_offset=None,
                        in_=net.chunks, in_offset=bass.IndirectOffsetOnAxis(ap=net.chunk_i[:, g:g + 1], axis=0),
                    ).then_inc(net.picked.sem, 16)
                pool.wait_ge(net.picked.sem, net.picked.after(16 * RG))

            @block.sync
            def _(sp):
                sp.wait_ge(net.dve_done.sem, net.dve_done.after(4))
                sp.dma_start(net.tile_row.rearrange("(g p) -> g p", p=P), tile_w[:, :]).then_inc(net.stored.sem, 16)
                sp.wait_ge(net.stored.sem, net.stored.after(16))
                sp.dma_start(net.tile_t[0:1, GS:GS + net.S], net.tile_row[0:net.S].rearrange("(p q) -> p q", p=1)
                             ).then_inc(net.stored.sem, 16)
                sp.wait_ge(net.stored.sem, net.stored.after(32))

            @block.scalar
            def _(act):
                act.memzero(net.tile_t[0:1, 0:GS]).then_inc(net.act_done.sem, 1)
    net.dve_done.passed(4)
    net.pe_done.passed(RG + 1)
    net.picked.passed(16 * RG)
    net.stored.passed(32)
    net.act_done.passed(1)


def edge_fields(net):
    nc, RG, VR, S = net.nc, net.RG, net.VR, net.S
    rows = [P] * (RG - 1) + [S - P * (RG - 1)]
    with ExitStack() as sc:
        names = ["src", "pidx", "dloc", "typ", "w", "slo", "shi"]
        F = {n: net.sb(sc, f"row_{n}", [P, RG, P]) for n in names if n != "w"}
        F["w"] = VR[:, :, 3, :].bitcast(F32)
        t1 = net.sb(sc, "row_t1", [P, RG, P])
        real = net.sb(sc, "row_real", [P, RG, P])
        inr = net.sb(sc, "row_in", [P, RG, P])
        flag = net.sb(sc, "row_flag", [P, RG, P])
        hole = net.sb(sc, "row_hole", [P, RG, P])
        styp = net.sb(sc, "row_styp", [P, RG, P])
        ri = net.sb(sc, "row_i", [P, RG, P], I32)
        pt = net.ps(sc, "ptf", [P, 2, 512])
        dest = {"src": net.src_i, "pidx": net.pidx_i, "dloc": net.dloc, "typ": net.typ, "w": net.w,
                "slo": net.slo, "shi": net.shi}
        with nc.Block() as block:
            @block.vector
            def _(dve):
                link = net.dve.on(dve)
                for b in dest.values():
                    link(dve.memset(b[:, S:S + AHEAD], 0))
                src, dloc = F["src"], F["dloc"]
                link(dve.tensor_copy(src[:, :, :], VR[:, :, 0, :]))
                link(dve.tensor_copy(F["typ"][:, :, :], VR[:, :, 2, :]))
                link(dve.scalar_tensor_tensor(out=F["pidx"][:, :, :], in0=src[:, :, :], scalar=float(net.R),
                                              in1=F["typ"][:, :, :], op0=ALU.mult, op1=ALU.add))
                link(dve.tensor_copy(t1[:, :, :], VR[:, :, 1, :]))
                link(dve.tensor_scalar(real[:, :, :], t1[:, :, :], float(net.N), None, ALU.is_lt))
                link(dve.tensor_copy(flag[:, :, :], VR[:, :, 4, :]))
                link(dve.tensor_tensor(flag[:, :, :], flag[:, :, :], t1[:, :, :], ALU.not_equal))
                link(dve.tensor_tensor(dloc[:, :, :], t1[:, :, :], wide(net.base128[:, :], 2, P), ALU.subtract))
                link(dve.tensor_scalar(t1[:, :, :], dloc[:, :, :], 0.0, None, ALU.is_ge))
                link(dve.scalar_tensor_tensor(out=inr[:, :, :], in0=dloc[:, :, :], scalar=float(P),
                                              in1=t1[:, :, :], op0=ALU.is_lt, op1=ALU.mult))
                link(dve.tensor_tensor(real[:, :, :], real[:, :, :], inr[:, :, :], ALU.mult))
                link(dve.scalar_tensor_tensor(out=flag[:, :, :], in0=flag[:, :, :], scalar=-BIG,
                                              in1=inr[:, :, :], op0=ALU.mult, op1=ALU.mult))
                link(dve.tensor_scalar(hole[:, :, :], inr[:, :, :], BIG, -BIG, ALU.mult, ALU.add))
                link(dve.tensor_scalar(t1[:, :, :], inr[:, :, :], -99.0, 99.0, ALU.mult, ALU.add))
                link(dve.tensor_tensor(styp[:, :, :], F["typ"][:, :, :], t1[:, :, :], ALU.add))
                link(dve.tensor_scalar(ri[:, :, :], VR[:, :, 0, :], P - 1, None, ALU.bitwise_and))
                link(dve.tensor_copy(t1[:, :, :], ri[:, :, :]))
                link(dve.scalar_tensor_tensor(out=t1[:, :, :], in0=t1[:, :, :], scalar=1.0,
                                              in1=real[:, :, :], op0=ALU.add, op1=ALU.mult))
                link(dve.tensor_scalar(F["slo"][:, :, :], t1[:, :, :], -1.0, None, ALU.add))
                link(dve.tensor_scalar(ri[:, :, :], VR[:, :, 0, :], 7, None, ALU.logical_shift_right))
                dve.tensor_copy(F["shi"][:, :, :], ri[:, :, :]).then_inc(net.dve_done.sem, 1)
                for k, n in enumerate(names):
                    for h in range(2):
                        dve.wait_ge(net.pe_done.sem, net.pe_done.after(2 * k + h + 1))
                        a = h * 512
                        b = min(S, a + 512)
                        dve.tensor_copy(dest[n][:, a:b], pt[:, h, 0:b - a]).then_inc(net.dve_done.sem, 1)

            @block.tensor
            def _(pe):
                pe.wait_ge(net.dve_done.sem, net.dve_done.after(1))
                for k, n in enumerate(names):
                    for h in range(2):
                        if k:
                            pe.wait_ge(net.dve_done.sem, net.dve_done.after(1 + 2 * (k - 1) + h + 1))
                        groups = range(4 * h, min(RG, 4 * h + 4))
                        for g in groups:
                            r = rows[g]
                            ins = pe.transpose(pt[:, h, (g % 4) * P:(g % 4) * P + r], F[n][0:r, g, :],
                                               net.ident[0:r, 0:r])
                        ins.then_inc(net.pe_done.sem, 1)

            @block.sync
            def _(sp):
                sp.wait_ge(net.dve_done.sem, net.dve_done.after(1))
                for k, b in enumerate((flag, hole, styp)):
                    sp.dma_start(net.lin[k, 0:RG * P * P].rearrange("(g p q) -> p g q", p=P, q=P),
                                 b[:, :, :]).then_inc(net.stored.sem, 16)
                sp.wait_ge(net.stored.sem, net.stored.after(48))
                V = net.V
                sp.dma_start(net.seg[0:P - 1, :], bass.AP(tensor=net.lin.tensor, offset=0,
                                                          ap=[[S, P - 1], [1, S + 1]])).then_inc(net.loaded.sem, 16)
                sp.dma_start(net.seg[P - 1:P, 0:S], net.lin[0, V - S:V].rearrange("(p q) -> p q", p=1)
                             ).then_inc(net.loaded.sem, 16)
                sp.dma_start(net.seg[P - 1:P, S:S + 1], net.lin[0, V - 1:V].rearrange("(p q) -> p q", p=1)
                             ).then_inc(net.loaded.sem, 16)
                for k, b in ((1, net.hole), (2, net.styp)):
                    sp.dma_start(b[:, :], net.lin[k, 0:V].rearrange("(p q) -> p q", p=P)).then_inc(net.loaded.sem, 16)
                sp.wait_ge(net.loaded.sem, net.loaded.after(80))
    net.dve_done.passed(1 + 2 * len(names))
    net.pe_done.passed(2 * len(names))
    net.stored.passed(48)
    net.loaded.passed(80)



def load_weights(net, a):
    L = 2
    net.vec, off = {}, 0
    rows = [("bq0", a["L0_gnn_Wq_b"]), ("bias0", a["L0_gnn_bias"]), ("gamma0", a["L0_gnn_ln_gamma"]),
            ("beta0", a["L0_gnn_ln_beta"]), ("b_in", a["L3_gnn_b_in"])]
    for l in range(L):
        rows += [((n, l), a[f"L3_gnn_{n}"][l]) for n in ("bq", "bk", "bv", "bskip")]
        rows += [(("We", l), a["L3_gnn_We"][l, 0]), (("Wbeta", l), a["L3_gnn_Wbeta"][l].rearrange("f a -> (f a)")),
                 (("gamma", l), a["L3_gnn_bn_gamma"][l]), (("beta", l), a["L3_gnn_bn_beta"][l])]
    mats = [("Wq0", a["L0_gnn_Wq_w"])] + [(f"Wk{i + 1}", a["L0_gnn_Wk_w"][i * D:(i + 1) * D, :]) for i in range(3)]
    mats += [("W_in", a["L3_gnn_W_in"])]
    for l in range(L):
        mats += [((n, l), a[f"L3_gnn_{n}"][l]) for n in ("Wq", "Wk", "Wv", "Wskip")]
    net.mat = {}
    with net.nc.Block() as block:
        @block.scalar
        def _(act):
            nonlocal off
            for name, v in rows:
                n = v.shape[0]
                net.vec[name] = net.VB[:, off:off + n]
                act.dma_start(net.VB[:, off:off + n], v.rearrange("(a n) -> a n", a=1).to_broadcast([P, n])
                              ).then_inc(net.weights_sem, 16)
                off += n
            for k, (name, m) in enumerate(mats):
                net.mat[name] = net.WB[:, k * D:(k + 1) * D]
                act.dma_start(net.WB[:, k * D:(k + 1) * D], m).then_inc(net.weights_sem, 16)
            act.dma_start(net.kb_col[:, :], a["L0_gnn_Wk_b"].rearrange("(p a) -> p a", a=1)
                          ).then_inc(net.weights_sem, 16)
            act.dma_start(net.rule_i[:, :], a["L0_gnn_rule_ids"].rearrange("(p a) -> p a", a=1)
                          ).then_inc(net.weights_sem, 16)
    net.weights_all = 16 * (len(rows) + len(mats) + 2)



def inverse_root(net, stat, tmp):
    with net.nc.Block() as block:
        @block.scalar
        def _(act):
            act.sqrt(tmp, stat).then_inc(net.act_done.sem, 1)

        @block.vector
        def _(dve):
            link = net.dve.on(dve)
            dve.wait_ge(net.act_done.sem, net.act_done.after(1))
            link(dve.reciprocal(tmp, tmp))
            link(dve.tensor_tensor(stat, stat, tmp, ALU.mult))
            link(dve.tensor_tensor(stat, stat, tmp, ALU.mult))
            link(dve.tensor_scalar(stat, stat, -0.5, 1.5, ALU.mult, ALU.add))
            link(dve.tensor_tensor(stat, stat, tmp, ALU.mult))
    net.act_done.passed(1)


def centre(net, src, dst, tmp, st):
    with net.nc.Block() as block:
        @block.vector
        def _(dve):
            link = net.dve.on(dve)
            link(dve.tensor_reduce(st[:, 0, :], src, AX, ALU.add))
            link(dve.tensor_scalar(st[:, 0, :], st[:, 0, :], -1.0 / D, None, ALU.mult))
            link(dve.tensor_tensor(tmp, src, wide(st[:, 0, :], 2, D), ALU.add))
            link(dve.tensor_tensor(dst, tmp, tmp, ALU.mult))
            link(dve.tensor_reduce(st[:, 1, :], dst, AX, ALU.add))
            link(dve.tensor_scalar(st[:, 1, :], st[:, 1, :], 1.0 / D, EPS, ALU.mult, ALU.add))
    inverse_root(net, st[:, 1, :], st[:, 0, :])


def norm_relu(net, src, dst, tmp, st):
    centre(net, src, dst, tmp, st)
    with net.nc.Block() as block:
        @block.vector
        def _(dve):
            link = net.dve.on(dve)
            link(dve.scalar_tensor_tensor(out=dst, in0=tmp, scalar=0.0, in1=wide(st[:, 1, :], 2, D),
                                          op0=ALU.max, op1=ALU.mult))


def turn_nodes(net, src, dst):
    NT = net.NT
    batches = [(b, min(NT, b + 4)) for b in range(0, NT, 4)]
    with ExitStack() as sc:
        pt = net.ps(sc, "turned", [P, 2, 512])
        with net.nc.Block() as block:
            @block.tensor
            def _(pe):
                for k, (a, b) in enumerate(batches):
                    if k >= 2:
                        pe.wait_ge(net.act_done.sem, net.act_done.after(k - 1))
                    for t in range(a, b):
                        ins = pe.transpose(pt[:, k % 2, (t - a) * P:(t - a + 1) * P], src[:, t, :], net.ident[:, :])
                    ins.then_inc(net.pe_done.sem, 1)

            @block.scalar
            def _(act):
                for k, (a, b) in enumerate(batches):
                    act.wait_ge(net.pe_done.sem, net.pe_done.after(k + 1))
                    act.copy(dst[:, a * P:b * P], pt[:, k % 2, 0:(b - a) * P]).then_inc(net.act_done.sem, 1)
    net.pe_done.passed(len(batches))
    net.act_done.passed(len(batches))


def project(net, hT, w, n, parts):
    NT = net.NT
    with ExitStack() as sc:
        BANKS = 4
        pt = net.ps(sc, "rows", [P, BANKS, 512])
        with net.nc.Block() as block:
            @block.tensor
            def _(pe):
                for t in range(NT):
                    if t >= BANKS:
                        pe.wait_ge(net.dve_done.sem, net.dve_done.after(len(parts) * (t - BANKS + 1)))
                    pe.matmul(pt[:, t % BANKS, 0:n], hT[:, t * P:(t + 1) * P], w, start=True,
                              stop=True).then_inc(net.pe_done.sem, 1)

            @block.vector
            def _(dve):
                for t in range(NT):
                    dve.wait_ge(net.pe_done.sem, net.pe_done.after(t + 1))
                    for a, b, to, plus in parts:
                        if plus is None:
                            ins = dve.tensor_copy(to(t), pt[:, t % BANKS, a:b])
                        else:
                            ins = dve.tensor_tensor(to(t), pt[:, t % BANKS, a:b], plus, ALU.add)
                        ins.then_inc(net.dve_done.sem, 1)
    net.pe_done.passed(NT)
    net.dve_done.passed(NT * len(parts))


def store_rows(net, pairs):
    with net.nc.Block() as block:
        @block.sync
        def _(sp):
            for table, rows in pairs:
                sp.dma_start(table.rearrange("(t p) d -> p t d", p=P), rows).then_inc(net.stored.sem, 16)
            sp.wait_ge(net.stored.sem, net.stored.after(16 * len(pairs)))
    net.stored.passed(16 * len(pairs))


def rule_terms(net, a, BX):
    R, NR = net.R, net.NR
    with ExitStack() as sc:
        rel = net.sb(sc, "h_rel", [P, R])
        hr = net.sb(sc, "h_rule", [NR, D])
        hrT = net.sb(sc, "h_ruleT", [P, NR])
        pt = net.ps(sc, "rules", [P, 512])
        with net.nc.Block() as block:
            @block.sync
            def _(sp):
                sp.dma_start(net.WR[:, :, :], a["L0_gnn_W_r"].rearrange("r d o -> d r o")).then_inc(net.loaded.sem, 16)
                sp.wait_ge(net.weights_sem, net.weights_all)
                sp.wait_ge(net.loaded.sem, net.loaded.after(16))

            @block.gpsimd
            def _(pool):
                pool.wait_ge(net.weights_sem, net.weights_all)
                pool.indirect_dma_start(out=hr[:, :], out_offset=None, in_=a["L0_gnn_rule_emb"],
                                        in_offset=bass.IndirectOffsetOnAxis(ap=net.rule_i[:, 0:1], axis=0)
                                        ).then_inc(net.picked.sem, 16)
                pool.wait_ge(net.picked.sem, net.picked.after(16))

            @block.vector
            def _(dve):
                link = net.dve.on(dve)
                dve.wait_ge(net.loaded.sem, net.loaded.after(16))
                link(dve.tensor_reduce(rel[:, :], net.WR[:, :, :], AX, ALU.add))
                dve.tensor_scalar(rel[:, :], rel[:, :], 1.0 / D, None, ALU.mult).then_inc(net.dve_done.sem, 1)
                dve.wait_ge(net.pe_done.sem, net.pe_done.after(1))
                dve.tensor_copy(hrT[:, :], pt[:, 0:NR]).then_inc(net.dve_done.sem, 1)
                dve.wait_ge(net.pe_done.sem, net.pe_done.after(3))
                link(dve.tensor_scalar(BX[:, 0:R], pt[:, 0:R], net.kb_col[:, 0:1], None, ALU.add))
                link(dve.tensor_copy(BX[:, R:R + NR], pt[:, R:R + NR]))

            @block.tensor
            def _(pe):
                pe.wait_ge(net.picked.sem, net.picked.after(16))
                pe.transpose(pt[:, 0:NR], hr[:, :], net.ident[0:NR, 0:NR]).then_inc(net.pe_done.sem, 1)
                pe.wait_ge(net.weights_sem, net.weights_all)
                pe.wait_ge(net.dve_done.sem, net.dve_done.after(2))
                pe.matmul(pt[:, 0:R], net.mat["Wk2"], rel[:, :], start=True, stop=True).then_inc(net.pe_done.sem, 1)
                pe.matmul(pt[:, R:R + NR], net.mat["Wk3"], hrT[:, :], start=True,
                          stop=True).then_inc(net.pe_done.sem, 1)
    net.loaded.passed(16)
    net.picked.passed(16)
    net.dve_done.passed(2)
    net.pe_done.passed(3)



def gather_rows(net, pool, taken, slots, indices, table, gathered, spilled=None):
    stage = net.index_stage

    def copy_indices(i, place):
        pool.tensor_copy(stage[:, place, :], indices[:, bass.ds(i * IT, IT)]).then_inc(net.staged.sem, 1)

    def iteration(i, place, last=False):
        for g in range(NG):
            n = i * NG + (g + 1)
            if g == 0:
                pool.wait_ge(net.staged.sem, net.staged.after(i + 1))
            pool.wait_ge(*taken(n))
            pool.sem_inc(net.pool_turn, 1)
            if spilled:
                pool.wait_ge(spilled.sem, spilled.after(n))
                pool.sem_inc(net.pool_turn, 1)
            if g == NG - 1 and not last:
                copy_indices(i + 1, 1 - place)
            for e in range(GS):
                k = g * GS + e
                pool.indirect_dma_start(out=slots[:, g, e, :], out_offset=None, in_=table,
                                        in_offset=bass.IndirectOffsetOnAxis(ap=stage[:, place, k:k + 1], axis=0)
                                        ).then_inc(gathered[g].sem, 16)

    copy_indices(0, 0)
    pairs = (net.ITERS - 1) // 2
    with pool.Fori(0, pairs) as j:
        iteration(2 * j, 0)
        iteration(2 * j + 1, 1)
    for i in range(2 * pairs, net.ITERS):
        iteration(i, i % 2, i == net.ITERS - 1)


def each_group(net, eng, body, iters=None):
    def iteration(i):
        for g in range(NG):
            body(i, g, i * NG + (g + 1), i * IT + g * GS)

    with eng.Fori(0, iters or net.ITERS) as i:
        iteration(i)
    if iters and iters < net.ITERS:
        for i in range(iters, net.ITERS):
            iteration(i)


class StepTiles:

    def __init__(self, net, eng, name):
        self.net, self.eng = net, eng
        self.regs = [eng.alloc_register(f"loop{net.loops}_{name}{e}") for e in range(GS)]

    def at(self, col):
        self.eng.load(self.regs, self.net.tile_t[0:1, bass.ds(col, GS)])
        return [self.eng.snap(r, min_val=0, max_val=self.net.NT - 1) for r in self.regs]

    def free(self):
        for r in self.regs:
            self.eng.free_register(r)


def onehots(net, dve, OH, col, slot):
    return dve.tensor_tensor(OH[:, slot, :, :], wide(net.iota[:, :], 1, GS),
                             wide(net.dloc[:, bass.ds(col, GS)], 2, P), ALU.is_equal)


def score_pass(net, kind, table, heads, hT=None, proj=None, v_rows=None):
    nc, S, R, NT = net.nc, net.S, net.R, net.NT
    rel = kind == "rel"
    XC = (R + net.NR) if rel else heads
    with ExitStack() as sc:
        K = net.sb(sc, "k_rows", [P, NG, GS, table.shape[1]])
        OH = net.sb(sc, "onehot", [P, NG, GS, P])
        OT = net.sb(sc, "onehotT", [P, 2, GS, P])
        PR = net.sb(sc, "products", [P, GS, D])
        R1 = net.sb(sc, "sums", [P, GS, heads])
        net.index_stage = net.sb(sc, "index_stage", [P, 2, IT], I32)
        pT = [net.ps(sc, f"pT{b}", [P, GS, P]) for b in range(2)]
        pQX = [net.ps(sc, f"pQX{b}", [P, GS, 256]) for b in range(2)]
        gathered = net.gather_sems()
        sem = net.loop_sem
        onehot_ready, turned, copied = sem("onehot_ready"), sem("turned"), sem("turned_copied")
        if rel:
            TY = net.sb(sc, "onehot_type", [P, GS, R])
            TX = net.sb(sc, "type_terms", [P, GS, R])
            R2 = net.sb(sc, "type_sums", [P, GS])
            LO = net.sb(sc, "onehot_src_lo", [P, 2, GS, P])
            HI = net.sb(sc, "onehot_src_hi", [P, 2, GS, NT])
            HS = net.sb(sc, "h_tile", [P, P])
            PO = net.sb(sc, "proj_rows", [P, NG, 512])
            pP = net.ps(sc, "pP", [P, 512])
            pH = net.ps(sc, "pH", [P, 512])
            vec = Progress(sem("scored"), ["onehot_type", "product", "type_terms", "taken", "sum", "type_sum",
                                           "score"])
            src_ready = sem("src_onehot_ready")
            mm = Progress(sem("expanded"), ["expanded", "counted"])
            proj_made, proj_copied = sem("proj_made"), sem("proj_copied")
            tile_placed, proj_free = sem("h_tile_placed"), sem("proj_slot_free")
            proj_stored = [sem(f"proj_stored{g}") for g in range(NG)]
            per_tile = R * D // (512 * NG)
            PI = NT * per_tile
            projv = proj.rearrange("(n r) o -> n (r o)", r=R)
            WRf = net.WR[:, :, :].rearrange("p r o -> p (r o)")
        else:
            spilled = sem("v_slot_spilled")
            v_stored = [sem(f"v_stored{g}") for g in range(NG)]
            TX = net.sb(sc, "weight_terms", [P, GS, heads])
            vec = Progress(sem("scored"), ["product", "taken", "sum", "score"])
            mm = Progress(sem("expanded"), ["expanded"])
            PI = None

        def makes_proj(i):
            return rel and not (isinstance(i, int) and i >= PI)

        with nc.Block() as block:
            @block.gpsimd
            def _(pool):
                gather_rows(net, pool, lambda n: (vec.sem, vec.at(n - NG, "taken")), K, net.src_i, table, gathered,
                            None if rel else spilled)

            @block.tensor
            def _(pe):
                mm.credit(pe)
                tiles = StepTiles(net, pe, "tile")

                def turn(n, slot, b):
                    pe.wait_ge(onehot_ready.sem, onehot_ready.after(n))
                    for e in range(GS):
                        ins = pe.transpose(pT[b][:, e, :], OH[:, slot, e, :], net.ident[:, :])
                    ins.then_inc(turned.sem, 1)

                def body(i, g, n, col):
                    b = g % 2
                    if makes_proj(i):
                        pe.wait_ge(tile_placed.sem, tile_placed.after(i + 1))
                        pe.wait_ge(proj_copied.sem, proj_copied.after(n))
                        pe.matmul(pP[:, :], HS[:, :], WRf[:, bass.ds((i % per_tile) * (NG * 512) + g * 512, 512)],
                                  start=True, stop=True).then_inc(proj_made.sem, 1)
                    tile = tiles.at(col + GS)
                    pe.wait_ge(copied.sem, copied.after(n + 1))
                    pe.wait_ge(vec.sem, vec.at(n - 2, "taken"))
                    for e, t in enumerate(tile):
                        ins = pe.matmul(pQX[b][:, e, 0:D + XC], OT[:, b, e, :],
                                        net.QX[:, bass.ds(t, 1), 0:D + XC], start=True, stop=True)
                    ins.then_inc(*mm.did("expanded"))
                    turn(n + 1, (g + 1) % NG, 1 - b)
                    if rel:
                        pe.wait_ge(src_ready.sem, src_ready.after(n))
                        for e in range(GS):
                            ins = pe.matmul(pH[:, 0:NT], LO[:, b, e, :], HI[:, b, e, :], start=False,
                                            stop=False, skip_group_check=True)
                        ins.then_inc(*mm.did("counted"))

                if rel:
                    pe.sem_inc(proj_made.sem, 1)
                    pe.matmul(pH[:, 0:NT], net.zero[:, :], net.zero[:, 0:NT], start=True, stop=False,
                              skip_group_check=True)
                turn(1, 0, 0)
                each_group(net, pe, body, PI)
                if rel:
                    pe.matmul(pH[:, 0:NT], net.zero[:, :], net.zero[:, 0:NT], start=False, stop=True,
                              skip_group_check=True).then_inc(net.pe_done.sem, 1)

            @block.scalar
            def _(act):
                act.sem_inc(copied.sem, 1)
                if rel:
                    act.sem_inc(proj_copied.sem, 1)

                def body(i, g, n, col):
                    b = g % 2
                    if makes_proj(i) and g == 0:
                        act.wait_ge(proj_made.sem, proj_made.after(i * NG + 1))
                        act.sem_inc(net.act_turn, 1)
                        act.copy(HS[:, :], hT[:, bass.ds((i // per_tile) * P, P)]).then_inc(tile_placed.sem, 1)
                    act.wait_ge(turned.sem, turned.after(n))
                    act.wait_ge(mm.sem, mm.at(n - 2, "expanded"))
                    act.copy(OT[:, b, :, :], pT[b][:, :, :]).then_inc(copied.sem, 1)
                    if makes_proj(i):
                        act.wait_ge(proj_made.sem, proj_made.after(n + 1))
                        act.wait_ge(proj_free.sem, proj_free.after(n))
                        act.copy(PO[:, g, :], pP[:, :]).then_inc(proj_copied.sem, 1)

                each_group(net, act, body, PI)

            @block.sync
            def _(sp):
                if not rel:
                    sp.sem_inc(spilled.sem, NG)

                    def spill(i, g, n, col):
                        sp.wait_ge(gathered[g].sem, gathered[g].after(64 * i + 64))
                        sp.dma_start(v_rows[bass.ds((i * NG + g) * P, P), :].rearrange("p (e d) -> p e d", d=D),
                                     K[:, g, :, D:2 * D]).then_inc(v_stored[g].sem, 16)
                        sp.wait_ge(v_stored[g].sem, v_stored[g].after(16 * i + 16))
                        sp.sem_inc(spilled.sem, 1)

                    each_group(net, sp, spill)
                    return
                sp.sem_inc(proj_free.sem, NG)

                def body(i, g, n, col):
                    if not makes_proj(i):
                        return
                    sp.wait_ge(proj_copied.sem, proj_copied.after(n + 1))
                    sp.dma_start(projv[bass.ds((i // per_tile) * P, P),
                                       bass.ds((i % per_tile) * (NG * 512) + g * 512, 512)],
                                 PO[:, g, :]).then_inc(proj_stored[g].sem, 16)
                    sp.wait_ge(proj_stored[g].sem, proj_stored[g].after(16 * i + 16))
                    sp.sem_inc(proj_free.sem, 1)

                each_group(net, sp, body, PI)

            @block.vector
            def _(dve):
                vec.credit(dve)
                onehots(net, dve, OH, 0, 0).then_inc(onehot_ready.sem, 1)
                onehots(net, dve, OH, GS, 1).then_inc(onehot_ready.sem, 1)

                def src_onehots(cols, b):
                    dve.tensor_tensor(LO[:, b, :, :], wide(net.iota[:, :], 1, GS), wide(net.slo[:, cols], 2, P),
                                      ALU.is_equal)
                    dve.tensor_tensor(HI[:, b, :, :], wide(net.iota[:, 0:NT], 1, GS), wide(net.shi[:, cols], 2, NT),
                                      ALU.is_equal).then_inc(src_ready.sem, 1)

                if rel:
                    src_onehots(slice(0, GS), 0)

                def body(i, g, n, col):
                    b = g % 2
                    cols = bass.ds(col, GS)
                    px = pQX[b][:, :, D:D + XC]
                    dve.wait_ge(vec.sem, vec.at(n - 1, "score"))
                    if rel:
                        dve.tensor_tensor(TY[:, :, :], wide(net.iota[:, 0:R], 1, GS), wide(net.typ[:, cols], 2, R),
                                          ALU.is_equal).then_inc(*vec.did("onehot_type"))
                    dve.wait_ge(gathered[g].sem, gathered[g].after(64 * i + 64))
                    dve.wait_ge(mm.sem, mm.at(n, "expanded"))
                    dve.tensor_tensor(PR[:, :, :], K[:, g, :, 0:D], pQX[b][:, :, 0:D], ALU.mult
                                      ).then_inc(*vec.did("product"))
                    if rel:
                        dve.wait_ge(vec.sem, vec.at(n, "onehot_type"))
                        dve.tensor_tensor(TX[:, :, :], TY[:, :, :], px[:, :, 0:R], ALU.mult
                                          ).then_inc(*vec.did("type_terms"))
                        dve.tensor_copy(net.rule[:, cols, :], px[:, :, R:XC]).then_inc(*vec.did("taken"))
                        dve.wait_ge(vec.sem, vec.at(n, "type_terms"))
                        dve.tensor_reduce(R1[:, :, 0], PR[:, :, :], AX, ALU.add).then_inc(*vec.did("sum"))
                        dve.tensor_reduce(R2[:, :], TX[:, :, :], AX, ALU.add).then_inc(*vec.did("type_sum"))
                    else:
                        dve.tensor_tensor(TX[:, :, :], px, wide(net.w[:, cols], 2, heads), ALU.mult
                                          ).then_inc(*vec.did("taken"))
                        dve.wait_ge(vec.sem, vec.at(n, "product"))
                        dve.tensor_reduce(R1[:, :, :], PR[:, :, :].rearrange("p e (h c) -> p e h c", h=heads),
                                          AX, ALU.add).then_inc(*vec.did("sum"))
                    onehots(net, dve, OH, col + 2 * GS, (g + 2) % NG).then_inc(onehot_ready.sem, 1)
                    if rel:
                        dve.wait_ge(mm.sem, mm.at(n - 1, "counted"))
                        src_onehots(bass.ds(col + GS, GS), 1 - b)
                        dve.wait_ge(vec.sem, vec.at(n, "type_sum"))
                        dve.tensor_tensor(net.score[:, cols], R1[:, :, 0], R2[:, :], ALU.add
                                          ).then_inc(*vec.did("score"))
                    else:
                        dve.wait_ge(vec.sem, vec.at(n, "sum"))
                        dve.tensor_tensor(net.score[:, cols, :], R1[:, :, :], TX[:, :, :], ALU.add
                                          ).then_inc(*vec.did("score"))

                each_group(net, dve, body)
                if rel:
                    dve.wait_ge(net.pe_done.sem, net.pe_done.after(1))
                    dve.tensor_copy(net.hist[:, :], pH[:, 0:NT]).then_inc(net.dve.sem, 1)
                    net.dve.n += 1
                    dve.wait_ge(net.dve.sem, net.dve.n)
        if rel:
            net.pe_done.passed(1)


def sum_pass(net, kind, width, table=None, indices=None, heads=0, v_rows=None):
    nc, S, R, NT, NR = net.nc, net.S, net.R, net.NT, net.NR
    gathers, typed = table is not None, kind in ("mass", "rel")
    rows_in = 16 if v_rows is not None else 64
    with ExitStack() as sc:
        acc = [net.acc, net.sb(sc, "acc_odd", [P, NT, W_ACC])]
        OH = net.sb(sc, "onehot", [P, NG, GS, P])
        V = net.sb(sc, "rows", [P, NG, GS, D]) if kind != "mass" else None
        M = net.sb(sc, "summands", [P, 2, GS, width]) if kind != "plain" else None
        if typed:
            TY = net.sb(sc, "onehot_type", [P, GS, R])
        if kind == "rel":
            OT = net.sb(sc, "onehotT", [P, 2, GS, P])
            E4 = net.sb(sc, "typed_exp", [P, GS, R, NR])
            AT = net.sb(sc, "typed_share", [P, GS, R * NR])
            AV = net.sb(sc, "attention", [P, 2, GS])
            pT = [net.ps(sc, f"pT{b}", [P, GS, P]) for b in range(2)]
            pR = [net.ps(sc, f"pR{b}", [P, GS, R * NR]) for b in range(2)]
        net.index_stage = net.sb(sc, "index_stage", [P, 2, IT], I32)
        pA = [net.ps(sc, f"pA{b}", [P, 2, 512]) for b in range(2)]
        gathered = net.gather_sems()
        sem = net.loop_sem
        onehot_ready = sem("onehot_ready")
        adds = [f"add{e}" for e in range(GS)]
        made = {"mass": ["onehot_type", "summands"], "rel": ["onehot_type", "typed_exp", "share", "attention"],
                "plain": [], "conv": ["summands", "weights"]}[kind]
        vec = Progress(sem("vector_summed"), made + adds)
        mm = Progress(sem("matrix_summed"), (["expanded"] if kind == "rel" else []) + ["aggregated"])
        if kind == "rel":
            rows = Progress(sem("rows_weighed"), ["rows"])
            turned, copied = sem("turned"), sem("turned_copied")
        with nc.Block() as block:
            @block.vector
            def _(dve):
                link = net.dve.on(dve)
                for a in acc:
                    link(dve.memset(a[:, :, :], 0.0))
                link(dve.memset(OH[:, NG - 1, :, :], 0.0))
                if M is not None:
                    link(dve.memset(M[:, :, :, :], 0.0))
                if kind == "rel":
                    link(dve.memset(M[:, :, :, D:D + 1], 1.0))
                if V is not None:
                    link(dve.memset(V[:, NG - 1, :, :], 0.0))

        with nc.Block() as block:
            if gathers:
                @block.gpsimd
                def _(pool):
                    taken = {"rel": lambda n: (rows.sem, rows.at(n - NG, "rows")),
                             "plain": lambda n: (mm.sem, mm.at(n - NG + 1, "aggregated"))}[kind]
                    gather_rows(net, pool, taken, V, indices, table, gathered)

            if v_rows is not None:
                @block.sync
                def _(sp):
                    def load(i, g, n, col):
                        sp.wait_ge(vec.sem, vec.at(n - NG, "summands"))
                        sp.dma_start(V[:, g, :, :], v_rows[bass.ds((i * NG + g) * P, P), :].rearrange(
                            "p (e d) -> p e d", d=D)).then_inc(gathered[g].sem, 16)

                    each_group(net, sp, load)

            @block.tensor
            def _(pe):
                mm.credit(pe)
                tiles = StepTiles(net, pe, "tile")

                def turn(n, slot, b):
                    pe.wait_ge(onehot_ready.sem, onehot_ready.after(n))
                    for e in range(GS):
                        ins = pe.transpose(pT[b][:, e, :], OH[:, slot, e, :], net.ident[:, :])
                    ins.then_inc(turned.sem, 1)

                def aggregate(g, n):
                    s, b = (g - 1) % NG, (g - 1) % 2
                    pe.wait_ge(vec.sem, vec.at(n - 2, adds[-1]))
                    if kind == "rel":
                        pe.wait_ge(rows.sem, rows.at(n - 1, "rows"))
                    elif made:
                        pe.wait_ge(vec.sem, vec.at(n - 1, made[-1]))
                    for e in range(GS):
                        row = M[:, b, e, :] if M is not None else V[:, s, e, :]
                        ins = pe.matmul(pA[b][:, e // 2, (e % 2) * 256:(e % 2) * 256 + width], OH[:, s, e, :],
                                        row, start=True, stop=True)
                    ins.then_inc(*mm.did("aggregated"))

                def body(i, g, n, col):
                    b = g % 2
                    if kind == "rel":
                        tile = tiles.at(col + GS)
                        pe.wait_ge(copied.sem, copied.after(n + 1))
                        pe.wait_ge(vec.sem, vec.at(n - 2, "share"))
                        for e, t in enumerate(tile):
                            ins = pe.matmul(pR[b][:, e, :], OT[:, b, e, :], net.QX[:, bass.ds(t, 1), 0:R * NR],
                                            start=True, stop=True)
                        ins.then_inc(*mm.did("expanded"))
                    else:
                        pe.wait_ge(onehot_ready.sem, onehot_ready.after(n))
                    if kind == "rel":
                        turn(n + 1, (g + 1) % NG, 1 - b)
                    aggregate(g, n)
                    if kind == "plain":
                        pe.wait_ge(gathered[g].sem, gathered[g].after(64 * i + 64))

                if kind == "rel":
                    turn(1, 0, 0)
                each_group(net, pe, body)
                if kind == "rel":
                    pe.wait_ge(mm.sem, mm.at(net.GROUPS, "aggregated"))
                    pe.sem_inc(*mm.did("expanded"))
                aggregate(0, net.GROUPS + 1)

            @block.vector
            def _(dve):
                vec.credit(dve)
                tiles = StepTiles(net, dve, "tile")
                onehots(net, dve, OH, 0, 0).then_inc(onehot_ready.sem, 1)
                onehots(net, dve, OH, GS, 1).then_inc(onehot_ready.sem, 1)

                def add(g, n, col):
                    b = (g - 1) % 2
                    tile = tiles.at(col)
                    dve.wait_ge(mm.sem, mm.at(n, "aggregated"))
                    for e, t in enumerate(tile):
                        to = acc[e % 2][:, bass.ds(t, 1), 0:width]
                        dve.wait_ge(vec.sem, vec.at(n, adds[e - 2]) if e >= 2 else vec.at(n - 1, adds[GS - 2 + e]))
                        dve.tensor_tensor(to, to, pA[b][:, e // 2, (e % 2) * 256:(e % 2) * 256 + width].unsqueeze(1),
                                          ALU.add).then_inc(*vec.did(adds[e]))

                def body(i, g, n, col):
                    b = g % 2
                    cols = bass.ds(col, GS)
                    if typed:
                        dve.tensor_tensor(TY[:, :, :], wide(net.iota[:, 0:R], 1, GS), wide(net.typ[:, cols], 2, R),
                                          ALU.is_equal).then_inc(*vec.did("onehot_type"))
                    dve.wait_ge(mm.sem, mm.at(n - 1, "aggregated"))
                    onehots(net, dve, OH, col + 2 * GS, (g + 2) % NG).then_inc(onehot_ready.sem, 1)
                    if typed:
                        dve.wait_ge(vec.sem, vec.at(n, "onehot_type"))
                        to = M[:, b, :, :].rearrange("p e (r a) -> p e r a", a=NR) if kind == "mass" else E4[:, :, :, :]
                        dve.tensor_tensor(to, wide(TY[:, :, :], 3, NR), wide(net.rule[:, cols, :], 2, R), ALU.mult
                                          ).then_inc(*vec.did("summands" if kind == "mass" else "typed_exp"))
                    if kind == "rel":
                        dve.wait_ge(vec.sem, vec.at(n, "typed_exp"))
                        dve.wait_ge(mm.sem, mm.at(n, "expanded"))
                        dve.tensor_tensor(AT[:, :, :], pR[b][:, :, :], E4[:, :, :, :].rearrange("p e r a -> p e (r a)"),
                                          ALU.mult).then_inc(*vec.did("share"))
                        dve.wait_ge(rows.sem, rows.at(n - 2, "rows"))
                        dve.wait_ge(vec.sem, vec.at(n, "share"))
                        dve.tensor_reduce(AV[:, b, :], AT[:, :, :], AX, ALU.add).then_inc(*vec.did("attention"))
                    if kind == "conv":
                        dve.wait_ge(gathered[g].sem, gathered[g].after(rows_in * i + rows_in))
                        c = D // heads
                        dve.sem_inc(net.dve_turn, 1)
                        dve.tensor_tensor(M[:, b, :, 0:D].rearrange("p e (h c) -> p e h c", h=heads),
                                          V[:, g, :, :].rearrange("p e (h c) -> p e h c", h=heads),
                                          wide(net.score[:, cols, :], 3, c), ALU.mult).then_inc(*vec.did("summands"))
                        dve.tensor_copy(M[:, b, :, D:D + heads], net.score[:, cols, :])
                        dve.tensor_copy(M[:, b, :, D + heads:D + 2 * heads], net.wscore[:, cols, :]
                                        ).then_inc(*vec.did("weights"))
                    add(g, n, col)

                each_group(net, dve, body)
                if made:
                    dve.wait_ge(vec.sem, vec.at(net.GROUPS, adds[-1]))
                for m in made:
                    dve.sem_inc(*vec.did(m))
                add(0, net.GROUPS + 1, net.S)
                dve.wait_ge(vec.sem, vec.at(net.GROUPS + 1, adds[-1]))
                net.dve.on(dve)(dve.tensor_tensor(acc[0][:, :, 0:width], acc[0][:, :, 0:width], acc[1][:, :, 0:width],
                                                  ALU.add))

            if kind == "rel":
                @block.scalar
                def _(act):
                    act.sem_inc(copied.sem, 1)
                    rows.credit(act)

                    def copy_turned(n, b):
                        act.wait_ge(turned.sem, turned.after(n))
                        act.wait_ge(mm.sem, mm.at(n - 2, "expanded"))
                        act.copy(OT[:, b, :, :], pT[b][:, :, :]).then_inc(copied.sem, 1)

                    copy_turned(1, 0)

                    def body(i, g, n, col):
                        b = g % 2
                        copy_turned(n + 1, 1 - b)
                        act.wait_ge(gathered[g].sem, gathered[g].after(64 * i + 64))
                        act.wait_ge(mm.sem, mm.at(n - 1, "aggregated"))
                        act.wait_ge(vec.sem, vec.at(n, "attention"))
                        for e in range(GS):
                            ins = act.activation(M[:, b, e, 0:D], V[:, g, e, :], ACT.Copy, scale=AV[:, b, e:e + 1])
                        ins.then_inc(*rows.did("rows"))

                    each_group(net, act, body)



def by_vector(net, work):
    with net.nc.Block() as block:
        @block.vector
        def _(dve):
            work(dve, net.dve.on(dve))


def row_groups(net):
    return [P] * (net.RG - 1) + [net.S - P * (net.RG - 1)]


def to_scan_layout(net, pairs):
    nc, RG, S, V = net.nc, net.RG, net.S, net.V
    full = (RG - 1) * P
    rest = S - full
    with ExitStack() as sc:
        RB = net.sb(sc, "rows_of_steps", [P, 2, RG, P])
        pt = [net.ps(sc, f"pt{k}", [P, 2, 512]) for k in range(2)]
        with nc.Block() as block:
            @block.tensor
            def _(pe):
                for k, (src, dst) in enumerate(pairs):
                    if k >= 2:
                        pe.wait_ge(net.act_done.sem, net.act_done.after(k - 1))
                    for g, r in enumerate(row_groups(net)):
                        ins = pe.transpose(pt[k % 2][0:r, g // 4, (g % 4) * P:(g % 4 + 1) * P],
                                           src[:, g * P:g * P + r], net.ident[:, :])
                    ins.then_inc(net.pe_done.sem, 1)

            @block.scalar
            def _(act):
                for k in range(len(pairs)):
                    act.wait_ge(net.pe_done.sem, net.pe_done.after(k + 1))
                    if k >= 2:
                        act.wait_ge(net.stored.sem, net.stored.after(32 * (k - 1)))
                    b = k % 2
                    act.copy(RB[:, b, 0:4, :], pt[b][:, 0, :].rearrange("p (g q) -> p g q", q=P))
                    act.copy(RB[:, b, 4:RG - 1, :], pt[b][:, 1, 0:(RG - 5) * P].rearrange("p (g q) -> p g q", q=P))
                    act.copy(RB[0:rest, b, RG - 1, :], pt[b][0:rest, 1, (RG - 5) * P:(RG - 4) * P]
                             ).then_inc(net.act_done.sem, 1)

            @block.sync
            def _(sp):
                for k, (src, dst) in enumerate(pairs):
                    sp.wait_ge(net.act_done.sem, net.act_done.after(k + 1))
                    sp.dma_start(net.lin[k, 0:full * P].rearrange("(g p q) -> p g q", p=P, q=P),
                                 RB[:, k % 2, 0:RG - 1, :]).then_inc(net.stored.sem, 16)
                    sp.dma_start(net.lin[k, full * P:V].rearrange("(p q) -> p q", q=P),
                                 RB[0:rest, k % 2, RG - 1, :]).then_inc(net.stored.sem, 16)
                    sp.wait_ge(net.stored.sem, net.stored.after(32 * (k + 1)))
                    sp.dma_start(dst, net.lin[k, 0:V].rearrange("(p q) -> p q", p=P)).then_inc(net.loaded.sem, 16)
                sp.wait_ge(net.loaded.sem, net.loaded.after(16 * len(pairs)))
    net.pe_done.passed(len(pairs))
    net.act_done.passed(len(pairs))
    net.stored.passed(32 * len(pairs))
    net.loaded.passed(16 * len(pairs))


def to_step_layout(net, pairs):
    nc, RG, S, V = net.nc, net.RG, net.S, net.V
    full = (RG - 1) * P
    rest = S - full
    with ExitStack() as sc:
        RB = net.sb(sc, "rows_of_steps", [P, 2, RG, P])
        pt = [net.ps(sc, f"pt{k}", [P, 2, 512]) for k in range(2)]
        with nc.Block() as block:
            @block.sync
            def _(sp):
                for k, (src, dst) in enumerate(pairs):
                    sp.dma_start(net.lin[k, 0:V].rearrange("(p q) -> p q", p=P), src).then_inc(net.stored.sem, 16)
                sp.wait_ge(net.stored.sem, net.stored.after(16 * len(pairs)))
                for k in range(len(pairs)):
                    if k >= 2:
                        sp.wait_ge(net.pe_done.sem, net.pe_done.after(k - 1))
                        sp.wait_ge(net.loaded.sem, net.loaded.after(32 * k))
                    sp.dma_start(RB[:, k % 2, 0:RG - 1, :],
                                 net.lin[k, 0:full * P].rearrange("(g p q) -> p g q", p=P, q=P)
                                 ).then_inc(net.loaded.sem, 16)
                    sp.dma_start(RB[0:rest, k % 2, RG - 1, :],
                                 net.lin[k, full * P:V].rearrange("(p q) -> p q", q=P)).then_inc(net.loaded.sem, 16)
                    if k % 2 == 0 and k + 1 < len(pairs):
                        sp.wait_ge(net.loaded.sem, net.loaded.after(32 * (k + 1)))

            @block.tensor
            def _(pe):
                for k in range(len(pairs)):
                    pe.wait_ge(net.loaded.sem, net.loaded.after(32 * (k + 1)))
                    if k >= 2:
                        pe.wait_ge(net.act_done.sem, net.act_done.after(k - 1))
                    for g, r in enumerate(row_groups(net)):
                        ins = pe.transpose(pt[k % 2][:, g // 4, (g % 4) * P:(g % 4) * P + r],
                                           RB[0:r, k % 2, g, :], net.ident[0:r, 0:r])
                    ins.then_inc(net.pe_done.sem, 1)

            @block.scalar
            def _(act):
                for k, (src, dst) in enumerate(pairs):
                    act.wait_ge(net.pe_done.sem, net.pe_done.after(k + 1))
                    act.copy(dst[:, 0:512], pt[k % 2][:, 0, :])
                    act.copy(dst[:, 512:S], pt[k % 2][:, 1, 0:S - 512]).then_inc(net.act_done.sem, 1)
    net.pe_done.passed(len(pairs))
    net.act_done.passed(len(pairs))
    net.stored.passed(16 * len(pairs))
    net.loaded.passed(32 * len(pairs))


class SegmentMax:

    def __init__(self, net, sc, channels):
        self.net, self.CH = net, channels
        self.start = net.sb(sc, "run_starts", [P, channels])
        self.first = net.sb(sc, "row_flags_right", [channels, P])
        self.second = net.sb(sc, "row_flags_left", [channels, P])
        self.carry = net.sb(sc, "row_states", [channels, P + 1])
        self.edge = net.sb(sc, "run_flags", [P, 2, channels])
        self.pt = net.ps(sc, "row_turned", [P, 512])
        self.pc = net.ps(sc, "run_turned", [P, 512])

    def flags(self):
        net, CH = self.net, self.CH
        with net.nc.Block() as block:
            @block.vector
            def _(dve):
                link = net.dve.on(dve)
                S = net.S
                for k in range(2):
                    link(dve.tensor_reduce(self.edge[:, k, 0:1], net.seg[:, k:k + S], AX, ALU.min))
                    dve.tensor_copy(self.edge[:, k, 1:CH], self.edge[:, k, 0:1].to_broadcast([P, CH - 1])
                                    ).then_inc(net.dve_done.sem, 1)
                for k, row in enumerate((self.first, self.second)):
                    dve.wait_ge(net.pe_done.sem, net.pe_done.after(k + 1))
                    link(dve.tensor_copy(row[:, :], (self.pt, self.pc)[k][0:CH, 0:P]))

            @block.tensor
            def _(pe):
                for k in range(2):
                    pe.wait_ge(net.dve_done.sem, net.dve_done.after(k + 1))
                    pe.transpose((self.pt, self.pc)[k][0:CH, 0:P], self.edge[:, k, :], net.ident[:, :]
                                 ).then_inc(net.pe_done.sem, 1)
        net.dve_done.passed(2)
        net.pe_done.passed(2)

    def vector(self, dve, link, X, Y, k=0):
        net, CH, S = self.net, self.CH, self.net.S
        right, left = net.seg[:, 0:S], net.seg[:, S:0:-1]
        done, turned = net.dve_done, net.pe_done

        def runs(to, flags, of, initial):
            for c in range(CH):
                ins = dve.tensor_tensor_scan(to(c), flags, of(c), initial(c), ALU.add, ALU.max)
            return ins

        def restart(n):
            dve.wait_ge(turned.sem, turned.after(4 * k + n))
            link(dve.tensor_copy(self.start[:, :], self.pc[:, 0:CH]))

        low = lambda c: -BIG
        begin = lambda c: self.start[:, c:c + 1]
        fy, fx = lambda c: Y[:, c, :], lambda c: X[:, c, :]
        by, bx = lambda c: Y[:, c, ::-1], lambda c: X[:, c, ::-1]
        runs(fy, right, fx, low).then_inc(done.sem, 1)
        link(dve.memset(self.carry[:, 0:1], -BIG))
        dve.wait_ge(turned.sem, turned.after(4 * k + 1))
        dve.tensor_tensor_scan(self.carry[:, 1:P + 1], self.first[:, :], self.pt[0:CH, 0:P], -BIG, ALU.add,
                               ALU.max).then_inc(done.sem, 1)
        restart(2)
        link(runs(fy, right, fx, begin))
        runs(bx, left, by, low).then_inc(done.sem, 1)
        link(dve.memset(self.carry[:, P:P + 1], -BIG))
        dve.wait_ge(turned.sem, turned.after(4 * k + 3))
        dve.tensor_tensor_scan(self.carry[:, P - 1::-1], self.second[:, ::-1], self.pt[0:CH, P - 1::-1], -BIG,
                               ALU.add, ALU.max).then_inc(done.sem, 1)
        restart(4)
        link(runs(bx, left, by, begin))

    def passed(self, uses):
        self.net.dve_done.passed(4 * uses)
        self.net.pe_done.passed(4 * uses)

    def tensor(self, pe, X, Y, k=0):
        net, CH, S = self.net, self.CH, self.net.S
        done, turned = net.dve_done, net.pe_done
        for j, (ends, of) in enumerate(((Y[:, :, S - 1], self.carry[:, 0:P]), (X[:, :, 0], self.carry[:, 1:P + 1]))):
            pe.wait_ge(done.sem, done.after(4 * k + 2 * j + 1))
            pe.transpose(self.pt[0:CH, 0:P], ends, net.ident[:, :]).then_inc(turned.sem, 1)
            pe.wait_ge(done.sem, done.after(4 * k + 2 * j + 2))
            pe.transpose(self.pc[:, 0:CH], of, net.ident[0:CH, 0:CH]).then_inc(turned.sem, 1)


def relation_weights(net):
    nc, S, R, NR = net.nc, net.S, net.R, net.NR
    scale = float(1.0 / D ** 0.5)
    CH = 4
    APART = 2.0 ** 100
    with ExitStack() as sc:
        X = net.sb(sc, "masked", [P, CH, S])
        Y = net.sb(sc, "scanned", [P, CH, S])
        A = [net.sb(sc, f"apart{k}", [P, CH, S]) for k in range(2)]
        SS = net.sb(sc, "scan_score", [P, S])
        TOP = net.sb(sc, "top", [P, S])
        TM = net.sb(sc, "top_steps", [P, S])
        bias = net.sb(sc, "type_bias", [P, R])
        seg = SegmentMax(net, sc, CH)
        to_scan_layout(net, [(net.score[:, 0:S], SS[:, :])])
        seg.flags()

        def prepare(dve, link):
            link(dve.memset(TOP[:, :], -BIG))
            link(dve.tensor_scalar(bias[:, :], net.iota[:, 0:R], -APART, None, ALU.mult))
        by_vector(net, prepare)
        rounds = R // CH
        with nc.Block() as block:
            @block.scalar
            def _(act):
                for k in range(rounds):
                    if k >= 2:
                        act.wait_ge(net.dve_rounds.sem, net.dve_rounds.after(k - 1))
                    for c in range(CH):
                        r = k * CH + c
                        ins = act.activation(A[k % 2][:, c, :], net.styp[:, :], ACT.Abs, bias=bias[:, r:r + 1],
                                             scale=APART)
                    ins.then_inc(net.act_done.sem, 1)

            @block.tensor
            def _(pe):
                for k in range(rounds):
                    seg.tensor(pe, X, Y, k)

            @block.vector
            def _(dve):
                link = net.dve.on(dve)
                for k in range(rounds):
                    apart = A[k % 2][:, :, :]
                    dve.wait_ge(net.act_done.sem, net.act_done.after(k + 1))
                    link(dve.tensor_tensor(X[:, :, :], wide(SS[:, :], 1, CH), apart, ALU.subtract))
                    seg.vector(dve, link, X, Y, k)
                    dve.tensor_tensor(X[:, :, :], X[:, :, :], apart, ALU.subtract).then_inc(net.dve_rounds.sem, 1)
                    dve.wait_ge(net.dve_rounds.sem, net.dve_rounds.after(k + 1))
                    for c in range(CH):
                        link(dve.tensor_tensor(TOP[:, :], TOP[:, :], X[:, c, :], ALU.max))
        net.act_done.passed(rounds)
        net.dve_rounds.passed(rounds)
        seg.passed(rounds)
        to_step_layout(net, [(TOP[:, :], TM[:, :])])

        def shift(dve, link):
            xs = X[:, :, :].rearrange("p c s -> p (c s)").rearrange("p (s c) -> p s c", c=NR)
            rule = net.rule[:, 0:S, :]
            link(dve.tensor_tensor(xs, rule, wide(TM[:, :], 2, NR), ALU.add))
            link(dve.tensor_scalar(xs, xs, scale, None, ALU.mult))
            link(dve.tensor_tensor(rule, rule, wide(net.score[:, 0:S], 2, NR), ALU.add))
            link(dve.scalar_tensor_tensor(out=rule, in0=rule, scalar=scale, in1=xs, op0=ALU.mult, op1=ALU.subtract))
            link(dve.tensor_scalar(rule, rule, 0.0, None, ALU.min))
        by_vector(net, shift)
        exp_in_place(net, net.rule[:, 0:S, :])


def exp_in_place(net, ap, scale=1.0):
    with net.nc.Block() as block:
        @block.scalar
        def _(act):
            act.activation(ap, ap, ACT.Exp, scale=scale).then_inc(net.act_done.sem, 1)
            act.wait_ge(net.act_done.sem, net.act_done.after(1))
    net.act_done.passed(1)


def head_weights(net):
    nc, S, H = net.nc, net.S, net.HEADS
    scale = float(1.0 / (D // H) ** 0.5)
    with ExitStack() as sc:
        X = net.sb(sc, "head_scores", [P, H, S])
        Y = net.sb(sc, "scanned", [P, H, S])
        seg = SegmentMax(net, sc, H)
        score = net.score[:, 0:S, :]
        by_vector(net, lambda dve, link: link(dve.tensor_scalar(score, score, scale, None, ALU.mult)))
        to_scan_layout(net, [(net.score[:, 0:S, h], X[:, h, :]) for h in range(H)])
        seg.flags()
        with nc.Block() as block:
            @block.tensor
            def _(pe):
                seg.tensor(pe, X, Y)

            @block.vector
            def _(dve):
                link = net.dve.on(dve)
                link(dve.tensor_tensor(X[:, :, :], X[:, :, :], wide(net.hole[:, :], 1, H), ALU.add))
                seg.vector(dve, link, X, Y)
        seg.passed(1)
        top = Y[:, :, :].rearrange("p h s -> p (h s)").rearrange("p (s h) -> p s h", h=H)
        to_step_layout(net, [(X[:, h, :], top[:, :, h]) for h in range(H)])

        def shift(dve, link):
            link(dve.tensor_tensor(score, score, top, ALU.subtract))
            link(dve.tensor_scalar(score, score, 0.0, None, ALU.min))
        by_vector(net, shift)
        exp_in_place(net, score)
        by_vector(net, lambda dve, link: link(dve.tensor_tensor(
            net.wscore[:, 0:S, :], score, wide(net.w[:, 0:S], 2, H), ALU.mult)))


def build(nc, a, out):
    N, E, R = a["x"].shape[0], a["src"].shape[0], a["L0_gnn_W_r"].shape[0]
    with ExitStack() as ctx:
        net = Net(nc, ctx, N, E, R)
        NT, S, RG = net.NT, net.S, net.RG
        sb = lambda name, shape, dt=F32: net.sb(ctx, name, shape, dt)
        net.X = sb("X", [P, NT, D])
        net.ident = sb("ident", [P, P])
        net.ones = sb("ones", [P, P])
        net.iota = sb("iota", [P, P])
        net.tile_t = sb("tile_t", [1, GS + S], I32)
        net.src_i = sb("src_i", [P, S + AHEAD], I32)
        net.pidx_i = sb("pidx_i", [P, S + AHEAD], I32)
        net.dloc = sb("dloc", [P, S + AHEAD])
        net.typ = sb("typ", [P, S + AHEAD])
        net.w = sb("w", [P, S + AHEAD])
        net.slo = sb("slo", [P, S + AHEAD])
        net.shi = sb("shi", [P, S + AHEAD])
        net.seg = sb("seg", [P, S + 1])
        net.hole = sb("hole", [P, S])
        net.styp = sb("styp", [P, S])
        net.NR = a["L0_gnn_rule_ids"].shape[0]
        net.VB = sb("weight_rows", [P, 3200])
        net.WB = sb("weight_mats", [P, 13 * D])
        net.kb_col = sb("kb_col", [P, 1])
        net.rule_i = sb("rule_i", [net.NR, 1], I32)
        net.zero = sb("zero", [P, P])
        net.hist = sb("hist", [P, NT])
        net.acc = sb("acc", [P, NT, W_ACC])
        net.QX = sb("QX", [P, NT, D + R + net.NR])
        net.H = sb("H", [P, NT, D])
        net.st = sb("stats", [P, 2, NT])
        net.chunks = net.dram("chunks", [RG * P, 5 * P], I32)
        net.tile_row = net.dram("tile_row", [RG * P], I32)
        net.lin = net.dram("lin", [4, RG * P * P])
        with ExitStack() as sc:
            net.CR = net.sb(sc, "CR", [P, RG, 5, P], I32)
            net.VR = net.sb(sc, "VR", [P, RG, 5, P], I32)
            net.iota_i = net.sb(sc, "iota_i", [P, P], I32)
            net.step_i = net.sb(sc, "step_i", [P, RG], I32)
            net.step_f = net.sb(sc, "step_f", [P, RG])
            net.chunk_i = net.sb(sc, "chunk_i", [P, RG], I32)
            net.base128 = net.sb(sc, "base128", [P, RG])
            weight = a["edge_weight1"].rearrange("e a -> (e a)").bitcast(I32)
            load_weights(net, a)
            load_edges(net, a["src"], a["dst"], a["edge_type_32"], weight, a["x"])
            pair_steps(net)
            edge_fields(net)

        k_table = net.dram("k_table", [net.NP, D])
        proj = net.dram("proj_table", [net.NP * R, D])
        with ExitStack() as l0:
            net.rule = net.sb(l0, "rule_scores", [P, S + GS, net.NR])
            net.score = net.sb(l0, "scores", [P, S + GS])
            with ExitStack() as sc:
                net.WR = net.sb(sc, "W_r", [P, R, D])
                hT = net.sb(sc, "hT", [P, net.NP])
                with ExitStack() as sc2:
                    BX = net.sb(sc2, "BX", [P, R + net.NR])
                    KN = net.sb(sc2, "node_tmp", [P, NT, D])
                    rule_terms(net, a, BX)
                    norm_relu(net, net.X[:, :, :], net.H[:, :, :], KN[:, :, :], net.st)
                    turn_nodes(net, net.H, hT)
                    project(net, hT, net.WB[:, 0:2 * D], 2 * D, [
                        (0, D, lambda t: net.QX[:, t, 0:D], net.vec["bq0"]),
                        (D, 2 * D, lambda t: KN[:, t, :], None)])
                    store_rows(net, [(k_table, KN[:, :, :])])
                    qT = KN[:, :, :].rearrange("p t d -> p (t d)")
                    turn_nodes(net, net.QX[:, :, 0:D], qT)
                    project(net, qT, BX[:, :], R + net.NR, [
                        (0, R + net.NR, lambda t: net.QX[:, t, D:D + R + net.NR], None)])
                score_pass(net, "rel", k_table, 1, hT, proj)
            relation_weights(net)
            sum_pass(net, "mass", R * net.NR)

            def inverse(dve, link):
                inv, mass = net.QX[:, :, 0:D], net.acc[:, :, 0:D]
                link(dve.tensor_scalar(mass, mass, 0.5, None, ALU.max))
                link(dve.reciprocal(inv, mass))
                link(dve.tensor_scalar(inv, inv, 1.0 / net.NR, None, ALU.mult))
            by_vector(net, inverse)
            sum_pass(net, "rel", D + 1, proj, net.pidx_i)

        in_deg = sb("in_degree", [P, NT])
        dis = sb("degree_roots", [P, NT])
        row = lambda v: wide(v, 1, NT)
        col = lambda s: wide(s, 2, D)
        acc, X, H, st = net.acc[:, :, 0:D], net.X[:, :, :], net.H[:, :, :], net.st

        with ExitStack() as sc:
            T = net.sb(sc, "node_tmp", [P, NT, D])

            def with_bias(dve, link):
                link(dve.tensor_copy(in_deg[:, :], net.acc[:, :, D]))
                link(dve.tensor_tensor(acc, acc, row(net.vec["bias0"]), ALU.add))
            by_vector(net, with_bias)
            centre(net, acc, H, T[:, :, :], st)

            def scale_add(dve, link):
                t = T[:, :, :]
                link(dve.tensor_tensor(t, t, col(st[:, 1, :]), ALU.mult))
                link(dve.tensor_tensor(t, t, row(net.vec["gamma0"]), ALU.mult))
                link(dve.tensor_tensor(t, t, row(net.vec["beta0"]), ALU.add))
                link(dve.tensor_scalar(t, t, 0.0, None, ALU.max))
                link(dve.tensor_tensor(X, X, t, ALU.add))
            by_vector(net, scale_add)

            table = net.dram("h_table", [net.NP, D])
            norm_relu(net, X, H, T[:, :, :], st)
            root = net.sb(sc, "root_tmp", [P, NT])
            by_vector(net, lambda dve, link: link(dve.tensor_scalar(dis[:, :], in_deg[:, :], 1.0, None, ALU.add)))
            inverse_root(net, dis[:, :], root[:, :])
            by_vector(net, lambda dve, link: link(dve.tensor_tensor(H, H, col(dis[:, :]), ALU.mult)))
            store_rows(net, [(table, H)])
        sum_pass(net, "plain", D, table, net.src_i)
        with ExitStack() as sc:
            T = net.sb(sc, "node_tmp", [P, NT, D])
            root = net.sb(sc, "root_tmp", [P, NT])
            by_vector(net, lambda dve, link: link(dve.tensor_scalar(dis[:, :], net.hist[:, :], 1.0, None, ALU.add)))
            inverse_root(net, dis[:, :], root[:, :])

            def residual(dve, link):
                link(dve.tensor_tensor(H, H, acc, ALU.add))
                link(dve.tensor_tensor(H, H, col(dis[:, :]), ALU.mult))
                link(dve.tensor_tensor(X, X, H, ALU.add))
            by_vector(net, residual)

            norm_relu(net, X, H, T[:, :, :], st)
            by_vector(net, lambda dve, link: link(dve.tensor_scalar(dis[:, :], net.hist[:, :], 1.0, None, ALU.max)))
            inverse_root(net, dis[:, :], root[:, :])
            by_vector(net, lambda dve, link: link(dve.tensor_tensor(H, H, col(dis[:, :]), ALU.mult)))
            store_rows(net, [(table, H)])
        sum_pass(net, "plain", D, table, net.src_i)

        net.HEADS = HD = 4
        kv_conv = net.dram("kv_conv", [net.NP, 2 * D])
        v_rows = net.dram("v_rows", [net.GROUPS * P, GS * D])
        XR = sb("skip", [P, NT, D])
        with ExitStack() as sc:
            T = net.sb(sc, "node_tmp", [P, NT, D])

            def residual2(dve, link):
                link(dve.tensor_tensor(acc, acc, col(dis[:, :]), ALU.mult))
                link(dve.tensor_tensor(X, X, acc, ALU.add))
            by_vector(net, residual2)

            norm_relu(net, X, T[:, :, :], H, st)
            hT = net.sb(sc, "hT", [P, net.NP])
            turn_nodes(net, T, hT)
            project(net, hT, net.mat["W_in"], D, [(0, D, lambda t: net.H[:, t, :], net.vec["b_in"])])
            by_vector(net, lambda dve, link: link(dve.tensor_scalar(H, H, 0.0, None, ALU.max)))

        for l in range(2):
            transformer_layer(net, l, XR, kv_conv, v_rows)

        by_vector(net, lambda dve, link: link(dve.tensor_tensor(X, X, H, ALU.add)))
        with nc.Block() as block:
            @block.sync
            def _(sp):
                full = (NT - 1) * P
                sp.dma_start(out[0:full, :].rearrange("(t p) d -> p t d", p=P), net.X[:, 0:NT - 1, :]
                             ).then_inc(net.stored.sem, 16)
                sp.dma_start(out[full:N, :], net.X[0:net.LAST, NT - 1, :]).then_inc(net.stored.sem, 16)
                sp.wait_ge(net.stored.sem, net.stored.after(32))


def transformer_layer(net, l, XR, kv_table, v_rows):
    nc, NT, HD = net.nc, net.NT, net.HEADS
    C = D // HD
    H, acc = net.H[:, :, :], net.acc[:, :, 0:D]
    row = lambda v: wide(v, 1, NT)
    col = lambda s: wide(s, 2, D)
    heads = lambda ap: ap.rearrange("p t (h c) -> p t h c", h=HD)
    We = net.vec[("We", l)]
    with ExitStack() as sc:
        KV = net.sb(sc, "kv_nodes", [P, NT, 2 * D])
        with ExitStack() as sc2:
            hT = net.sb(sc2, "hT", [P, net.NP])
            turn_nodes(net, net.H, hT)
            k = 5 + 4 * l
            project(net, hT, net.WB[:, k * D:(k + 4) * D], 4 * D, [
                (0, D, lambda t: net.QX[:, t, 0:D], net.vec[("bq", l)]),
                (D, 2 * D, lambda t: KV[:, t, 0:D], net.vec[("bk", l)]),
                (2 * D, 3 * D, lambda t: KV[:, t, D:2 * D], net.vec[("bv", l)]),
                (3 * D, 4 * D, lambda t: XR[:, t, :], net.vec[("bskip", l)])])
        store_rows(net, [(kv_table, KV[:, :, :])])

        def edge_term(dve, link):
            k = KV[:, :, 0:D]
            link(dve.tensor_tensor(k, net.QX[:, :, 0:D], row(We), ALU.mult))
            link(dve.tensor_reduce(net.QX[:, :, D:D + HD], heads(k), AX, ALU.add))
        by_vector(net, edge_term)
    with ExitStack() as sc:
        net.score = net.sb(sc, "head_score", [P, net.S, HD])
        net.wscore = net.sb(sc, "head_weight", [P, net.S, HD])
        score_pass(net, "conv", kv_table, HD, v_rows=v_rows)
        head_weights(net)
        sum_pass(net, "conv", D + 2 * HD, heads=HD, v_rows=v_rows)
    with ExitStack() as sc:
        T = net.sb(sc, "node_tmp", [P, NT, D])
        U = net.sb(sc, "node_tmp2", [P, NT, D])
        z = net.sb(sc, "gate", [P, NT])
        inv = net.sb(sc, "mass_inverse", [P, NT, HD])
        t, u, xr = T[:, :, :], U[:, :, :], XR[:, :, :]
        Wb = net.vec[("Wbeta", l)]

        def gate_logit(dve, link):
            wide_c = lambda s: wide(s, 3, C)
            We_h = wide(We.rearrange("p (h c) -> p h c", h=HD), 1, NT)
            link(dve.tensor_tensor(heads(t), We_h, wide_c(net.acc[:, :, D + HD:D + 2 * HD]), ALU.mult))
            link(dve.tensor_tensor(acc, acc, t, ALU.add))
            link(dve.tensor_scalar(inv[:, :, :], net.acc[:, :, D:D + HD], 0.5, None, ALU.max))
            link(dve.reciprocal(inv[:, :, :], inv[:, :, :]))
            link(dve.tensor_tensor(heads(acc), heads(acc), wide_c(inv[:, :, :]), ALU.mult))
            link(dve.tensor_tensor(t, acc, row(Wb[:, 0:D]), ALU.mult))
            link(dve.tensor_tensor(u, xr, row(Wb[:, D:2 * D]), ALU.mult))
            link(dve.tensor_tensor(t, t, u, ALU.add))
            link(dve.tensor_tensor(u, acc, xr, ALU.subtract))
            link(dve.tensor_tensor(u, u, row(Wb[:, 2 * D:3 * D]), ALU.mult))
            link(dve.tensor_tensor(t, t, u, ALU.add))
            link(dve.tensor_reduce(z[:, :], t, AX, ALU.add))
            link(dve.tensor_scalar(z[:, :], z[:, :], -80.0, None, ALU.max))
        by_vector(net, gate_logit)
        exp_in_place(net, z[:, :], scale=-1.0)

        def gated(dve, link):
            link(dve.tensor_scalar(z[:, :], z[:, :], 1.0, None, ALU.add))
            link(dve.reciprocal(z[:, :], z[:, :]))
            link(dve.tensor_tensor(t, xr, col(z[:, :]), ALU.mult))
            link(dve.tensor_scalar(z[:, :], z[:, :], -1.0, 1.0, ALU.mult, ALU.add))
            link(dve.tensor_tensor(acc, acc, col(z[:, :]), ALU.mult))
            link(dve.tensor_tensor(t, t, acc, ALU.add))
        by_vector(net, gated)
        batch_norm(net, T, U, net.vec[("gamma", l)], net.vec[("beta", l)])

        def activate(dve, link):
            link(dve.tensor_scalar(t, t, 0.0, None, ALU.max))
            link(dve.tensor_tensor(H, H, t, ALU.add))
        by_vector(net, activate)


def batch_norm(net, T, U, gamma, beta):
    NT, LAST = net.NT, net.LAST
    t, u = T[:, :, :], U[:, :, :]
    row = lambda v: wide(v, 1, NT)
    with ExitStack() as sc:
        mu = net.sb(sc, "mean", [P, D])
        var = net.sb(sc, "variance", [P, D])
        tmp = net.sb(sc, "root_tmp", [P, D])
        ps = net.ps(sc, "node_sums", [P, 2, 512])

        def sums(pe, src, k):
            for i in range(NT):
                n = P if i < NT - 1 else LAST
                ins = pe.matmul(ps[:, k, 0:D], net.ones[0:n, :], src[0:n, i, :], start=i == 0, stop=i == NT - 1)
            ins.then_inc(net.pe_done.sem, 1)

        with net.nc.Block() as block:
            @block.tensor
            def _(pe):
                sums(pe, T, 0)
                pe.wait_ge(net.dve_done.sem, net.dve_done.after(1))
                sums(pe, U, 1)

            @block.vector
            def _(dve):
                link = net.dve.on(dve)
                dve.wait_ge(net.pe_done.sem, net.pe_done.after(1))
                link(dve.tensor_scalar(mu[:, :], ps[:, 0, 0:D], 1.0 / net.N, None, ALU.mult))
                link(dve.tensor_tensor(t, t, row(mu[:, :]), ALU.subtract))
                dve.tensor_tensor(u, t, t, ALU.mult).then_inc(net.dve_done.sem, 1)
                dve.wait_ge(net.pe_done.sem, net.pe_done.after(2))
                link(dve.tensor_scalar(var[:, :], ps[:, 1, 0:D], 1.0 / net.N, EPS, ALU.mult, ALU.add))
        net.pe_done.passed(2)
        net.dve_done.passed(1)
        inverse_root(net, var[:, :], tmp[:, :])

        def scale(dve, link):
            link(dve.tensor_tensor(var[:, :], var[:, :], gamma, ALU.mult))
            link(dve.tensor_tensor(t, t, row(var[:, :]), ALU.mult))
            link(dve.tensor_tensor(t, t, row(beta), ALU.add))
        by_vector(net, scale)


def kernel(**inputs):
    import numpy as _np
    import concourse.bacc as _bacc
    from concourse import mybir as _mybir
    from concourse.bass_utils import run_bass_kernel_spmd as _run

    nc = _bacc.Bacc("TRN2", target_bir_lowering=False, num_devices=1)
    arrays, args = {}, {}
    for name, value in inputs.items():
        v = _np.ascontiguousarray(value)
        arrays[f"in_{name}"] = v
        args[name] = nc.dram_tensor(f"in_{name}", v.shape, _mybir.dt.from_np(v.dtype), kind="ExternalInput").ap()
    x = arrays["in_x"]
    out = nc.dram_tensor("out", x.shape, _mybir.dt.from_np(x.dtype), kind="ExternalOutput").ap()
    build(nc, args, out)
    r = _run(nc, [arrays], core_ids=[0])
    return r.results[0]["out"]
```

```python
from contextlib import ExitStack

import concourse.bass as bass
from concourse import mybir

F32 = mybir.dt.float32
I32 = mybir.dt.int32
ALU = mybir.AluOpType
ACT = mybir.ActivationFunctionType
AX = mybir.AxisListType.X

P = 128
D = 128
BIG = 1e30
EPS = 1e-5
GS = 4
NG = 4
IT = GS * NG
AHEAD = 2 * GS
W_ACC = 136


def ceil_div(a, b):
    return -(-a // b)


class Progress:
    DEPTH = 4

    def __init__(self, sem, actions):
        self.sem, self.actions, self.turn = sem.sem, list(actions), 0

    def credit(self, eng):
        eng.sem_inc(self.sem, self.DEPTH * len(self.actions))

    def at(self, group, action):
        k = len(self.actions)
        return (group + (self.DEPTH - 1)) * k + (self.actions.index(action) + 1)

    def did(self, action):
        assert self.actions[self.turn % len(self.actions)] == action, (action, self.turn)
        self.turn += 1
        return self.sem, 1


class Chain:

    def __init__(self, sem):
        self.sem, self.n = sem, 0

    def on(self, eng):
        def link(ins):
            self.n += 1
            ins.then_inc(self.sem, 1)
            eng.wait_ge(self.sem, self.n)
        return link


class Signal:

    def __init__(self, sem):
        self.sem, self.base = sem, 0

    def after(self, n):
        return self.base + n

    def passed(self, n):
        self.base += n


class Net:

    def __init__(self, nc, ctx, N, E, R):
        self.nc, self.ctx = nc, ctx
        self.N, self.E, self.R = N, E, R
        self.NT = ceil_div(N, P)
        self.NP = self.NT * P
        self.LAST = N - (self.NT - 1) * P
        self.C = ceil_div(E, P)
        self.GROUPS = ceil_div(self.C + self.NT - 1, GS)
        self.S = self.GROUPS * GS
        self.ITERS = ceil_div(self.GROUPS, NG)
        self.SP = max(self.S + AHEAD, self.ITERS * IT)
        self.RG = ceil_div(self.S, P)
        self.V = self.S * P
        sem = lambda name: ctx.enter_context(nc.semaphore(name))
        self.dve = Chain(sem("dve_chain"))
        self.pool = Chain(sem("pool_chain"))
        self.pe_done = Signal(sem("pe_done"))
        self.dve_done = Signal(sem("dve_done"))
        self.act_done = Signal(sem("act_done"))
        self.dve_rounds = Signal(sem("dve_rounds"))
        self.loaded = Signal(sem("loaded"))
        self.x_loaded = Signal(sem("x_loaded"))
        self.picked = Signal(sem("rows_picked"))
        self.stored = Signal(sem("stored"))
        self.plane_stored = [Signal(sem(f"plane_stored{k}")) for k in range(2)]
        self.weights_sem = sem("weights_loaded")
        self.pool_turn, self.act_turn, self.dve_turn = sem("pool_turn"), sem("act_turn"), sem("dve_turn")
        self.loops = 0
        self.used = {}

    def loop_sem(self, name):
        return Signal(self.ctx.enter_context(self.nc.semaphore(f"loop{self.loops}_{name}")))

    def gather_sems(self):
        self.loops += 1
        self.staged = self.loop_sem("indices_staged")
        return [self.loop_sem(f"gathered{g}") for g in range(NG)]

    def once(self, name):
        self.used[name] = self.used.get(name, 0) + 1
        return name if self.used[name] == 1 else f"{name}_{self.used[name]}"

    def sb(self, scope, name, shape, dt=F32):
        return scope.enter_context(self.nc.sbuf_tensor(self.once(name), shape, dt))

    def ps(self, scope, name, shape, dt=F32):
        return scope.enter_context(self.nc.psum_tensor(self.once(name), shape, dt))

    def dram(self, name, shape, dt=F32):
        return self.nc.dram_tensor(name, shape, dt).ap()


def wide(ap, at, n):
    u = ap.unsqueeze(at)
    shape = list(u.shape)
    shape[at] = n
    return u.to_broadcast(shape)



def load_edges(net, src, dst, typ, weight, x, issue_weights):
    nc, C, E = net.nc, net.C, net.E
    FULL = E // P
    G = FULL // P
    RF = FULL - G * P
    REST = E - FULL * P
    RG = net.RG
    CR = net.CR
    pad = net.NP - 1
    fields = [(src, 0), (dst, 1), (typ, 2), (weight, 3)]
    with nc.Block() as block:
        @block.vector
        def _(dve):
            dve.memset(net.X[:, net.NT - 1, :], 0.0)
            dve.memset(CR[:, :, 0, :], 0)
            dve.memset(CR[:, :, 2:4, :], 0)
            dve.memset(CR[:, :, 1, :], pad)
            dve.memset(CR[:, :, 4, :], pad).then_inc(net.dve_done.sem, 1)
            dve.memset(net.ones[:, :], 1.0)
            dve.memset(net.zero[:, :], 0.0)
            dve.memset(net.ident[:, :], 0.0).then_inc(net.dve_done.sem, 1)
            dve.wait_ge(net.x_loaded.sem, net.x_loaded.after(32))
            centre_rows(dve, net.dve.on(dve), net.X[:, :, :], net.H[:, :, :], net.acc[:, :, 0:D], net.st)

        @block.scalar
        def _(act):
            issue_weights(act)

        @block.sync
        def _(sp):
            n = 0

            def load(to, of):
                nonlocal n
                sp.dma_start(to, of).then_inc(net.loaded.sem, 16)
                n += 16

            sp.dma_start(net.X[:, 0:net.NT - 1, :], x[0:(net.NT - 1) * P, :].rearrange(
                "(t p) d -> p t d", p=P)).then_inc(net.x_loaded.sem, 16)
            sp.wait_ge(net.dve_done.sem, net.dve_done.after(1))
            sp.dma_start(net.X[0:net.LAST, net.NT - 1, :], x[(net.NT - 1) * P:net.N, :]
                         ).then_inc(net.x_loaded.sem, 16)
            for a, f in fields:
                load(CR[:, 0:G, f, :], a[0:G * P * P].rearrange("(g p q) -> p g q", p=P, q=P))
                load(CR[0:RF, G, f, :], a[G * P * P:FULL * P].rearrange("(p q) -> p q", q=P))
                if REST:
                    load(CR[RF:RF + 1, G, f, 0:REST], a[FULL * P:E].rearrange("(p q) -> p q", p=1))
            load(CR[0:1, 0, 4, 1:P], dst[0:P - 1].rearrange("(p q) -> p q", p=1))
            load(CR[1:P, 0, 4, :], dst[P - 1:P * P - 1].rearrange("(p q) -> p q", q=P))
            load(CR[:, 1:G, 4, :], dst[P * P - 1:G * P * P - 1].rearrange("(g p q) -> p g q", p=P, q=P))
            load(CR[0:RF, G, 4, :], dst[G * P * P - 1:FULL * P - 1].rearrange("(p q) -> p q", q=P))
            load(CR[RF:RF + 1, G, 4, 0:REST + 1], dst[FULL * P - 1:E].rearrange("(p q) -> p q", p=1))
            sp.wait_ge(net.loaded.sem, net.loaded.after(n))
            sp.dma_start(net.chunks.rearrange("(g p) f -> p g f", p=P),
                         CR[:, :, :, :].rearrange("p g f q -> p g (f q)")).then_inc(net.stored.sem, 16)
            sp.wait_ge(net.stored.sem, net.stored.after(16))
            net.loaded.passed(n)
            net.stored.passed(16)

        @block.gpsimd
        def _(pool):
            link = net.pool.on(pool)
            pool.wait_ge(net.dve_done.sem, net.dve_done.after(2))
            link(pool.affine_select(out=net.ident[:, :], in_=net.ident[:, :], compare_op=ALU.not_equal,
                                    fill=1.0, base=0, pattern=[[-1, P]], channel_multiplier=1))
            link(pool.iota(net.iota_i[:, :], pattern=[[1, P]], base=0, channel_multiplier=0))
            link(pool.tensor_copy(net.iota[:, :], net.iota_i[:, :]))
            link(pool.iota(net.step_i[:, :], pattern=[[P, RG]], base=0, channel_multiplier=1))
            link(pool.tensor_copy(net.step_f[:, :], net.step_i[:, :]))
    net.dve_done.passed(2)


def pair_steps(net):
    nc, RG, CR = net.nc, net.RG, net.CR
    KW = RG * P
    with ExitStack() as sc:
        last = net.sb(sc, "last_tile", [P, RG], I32)
        key = net.sb(sc, "chunk_key", [P, RG])
        keyw = net.sb(sc, "chunk_key_wide", [P, RG, P])
        keys = net.sb(sc, "keys_everywhere", [P, KW])
        below = net.sb(sc, "below", [P, KW])
        chunk_f = net.sb(sc, "chunk_f", [P, RG])
        tile_f = net.sb(sc, "tile_f", [P, RG])
        tile_w = net.sb(sc, "tile_w", [RG, P], I32)
        pk = net.ps(sc, "pk", [P, 2, 512])
        pt = net.ps(sc, "pt", [P, 512])
        with nc.Block() as block:
            @block.vector
            def _(dve):
                link = net.dve.on(dve)
                link(dve.tensor_scalar(last[:, :], CR[:, :, 1, P - 1], 7, None, ALU.logical_shift_right))
                link(dve.tensor_copy(key[:, :], last[:, :]))
                link(dve.tensor_tensor(key[:, :], key[:, :], net.step_f[:, :], ALU.add))
                dve.tensor_copy(keyw[:, :, :], wide(key[:, :], 2, P)).then_inc(net.dve_done.sem, 1)
                dve.wait_ge(net.pe_done.sem, net.pe_done.after(RG))
                link(dve.tensor_copy(keys[:, 0:512], pk[:, 0, :]))
                link(dve.tensor_copy(keys[:, 512:KW], pk[:, 1, 0:KW - 512]))
                for g in range(RG):
                    link(dve.tensor_tensor(below[:, :], keys[:, :],
                                           net.step_f[:, g:g + 1].to_broadcast([P, KW]), ALU.is_lt))
                    link(dve.tensor_reduce(chunk_f[:, g:g + 1], below[:, :], AX, ALU.add))
                link(dve.tensor_copy(net.chunk_i[:, :], chunk_f[:, :]))
                dve.tensor_tensor(tile_f[:, :], net.step_f[:, :], chunk_f[:, :],
                                  ALU.subtract).then_inc(net.dve_done.sem, 1)
                dve.wait_ge(net.dve_done.sem, net.dve_done.after(2))
                link(dve.tensor_scalar(tile_f[:, :], tile_f[:, :], float(net.NT - 1), None, ALU.min))
                dve.tensor_scalar(net.base128[:, :], tile_f[:, :], float(P), None,
                                  ALU.mult).then_inc(net.dve_done.sem, 1)
                dve.wait_ge(net.pe_done.sem, net.pe_done.after(RG + 1))
                dve.tensor_copy(tile_w[:, :], pt[0:RG, 0:P]).then_inc(net.dve_done.sem, 1)

            @block.tensor
            def _(pe):
                pe.wait_ge(net.dve_done.sem, net.dve_done.after(1))
                for g in range(RG):
                    pe.matmul(pk[:, g // 4, (g % 4) * P:(g % 4 + 1) * P], keyw[:, g, :], net.ident[:, :],
                              start=True, stop=True).then_inc(net.pe_done.sem, 1)
                pe.wait_ge(net.dve_done.sem, net.dve_done.after(3))
                pe.transpose(pt[0:RG, 0:P], tile_f[:, :], net.ident[:, :]).then_inc(net.pe_done.sem, 1)

            @block.gpsimd
            def _(pool):
                pool.wait_ge(net.dve_done.sem, net.dve_done.after(2))
                for g in range(RG):
                    pool.indirect_dma_start(
                        out=net.VR[:, g, :, :].rearrange("p f q -> p (f q)"), out_offset=None,
                        in_=net.chunks, in_offset=bass.IndirectOffsetOnAxis(ap=net.chunk_i[:, g:g + 1], axis=0),
                    ).then_inc(net.picked.sem, 16)
                pool.wait_ge(net.picked.sem, net.picked.after(16 * RG))

            @block.sync
            def _(sp):
                sp.wait_ge(net.dve_done.sem, net.dve_done.after(4))
                sp.dma_start(net.tile_row.rearrange("(g p) -> g p", p=P), tile_w[:, :]).then_inc(net.stored.sem, 16)
                sp.wait_ge(net.stored.sem, net.stored.after(16))
                sp.dma_start(net.tile_t[0:1, GS:GS + net.S], net.tile_row[0:net.S].rearrange("(p q) -> p q", p=1)
                             ).then_inc(net.stored.sem, 16)
                sp.wait_ge(net.stored.sem, net.stored.after(32))

            @block.scalar
            def _(act):
                act.memzero(net.tile_t[0:1, 0:GS]).then_inc(net.act_done.sem, 1)
    net.dve_done.passed(4)
    net.pe_done.passed(RG + 1)
    net.picked.passed(16 * RG)
    net.stored.passed(32)
    net.act_done.passed(1)


def edge_fields(net):
    nc, RG, VR, S = net.nc, net.RG, net.VR, net.S
    rows = [P] * (RG - 1) + [S - P * (RG - 1)]
    with ExitStack() as sc:
        names = ["w", "src", "typ", "pidx", "dloc", "slo", "shi"]
        made = {"w": 0, "src": 1, "typ": 1, "pidx": 1, "dloc": 2, "slo": 3, "shi": 3}
        F = {n: net.sb(sc, f"row_{n}", [P, RG, P]) for n in names if n != "w"}
        F["w"] = VR[:, :, 3, :].bitcast(F32)
        t1 = net.sb(sc, "row_t1", [P, RG, P])
        real = net.sb(sc, "row_real", [P, RG, P])
        inr = net.sb(sc, "row_in", [P, RG, P])
        flag = net.sb(sc, "row_flag", [P, RG, P])
        hole = net.sb(sc, "row_hole", [P, RG, P])
        styp = net.sb(sc, "row_styp", [P, RG, P])
        ri = net.sb(sc, "row_i", [P, RG, P], I32)
        pt = net.ps(sc, "ptf", [P, 2, 2, 512])
        dest = {"src": net.src_i, "pidx": net.pidx_i, "dloc": net.dloc, "typ": net.typ, "w": net.w,
                "slo": net.slo, "shi": net.shi}
        with nc.Block() as block:
            @block.vector
            def _(dve):
                link = net.dve.on(dve)
                for b in dest.values():
                    link(dve.memset(b[:, S:net.SP], 0))
                src, dloc = F["src"], F["dloc"]
                link(dve.tensor_copy(src[:, :, :], VR[:, :, 0, :]))
                link(dve.tensor_copy(F["typ"][:, :, :], VR[:, :, 2, :]))
                link(dve.scalar_tensor_tensor(out=F["pidx"][:, :, :], in0=src[:, :, :], scalar=float(net.R),
                                              in1=F["typ"][:, :, :], op0=ALU.mult, op1=ALU.add))
                dve.sem_inc(net.dve_done.sem, 1)
                link(dve.tensor_copy(t1[:, :, :], VR[:, :, 1, :]))
                link(dve.tensor_scalar(real[:, :, :], t1[:, :, :], float(net.N), None, ALU.is_lt))
                link(dve.tensor_copy(flag[:, :, :], VR[:, :, 4, :]))
                link(dve.tensor_tensor(flag[:, :, :], flag[:, :, :], t1[:, :, :], ALU.not_equal))
                link(dve.tensor_tensor(dloc[:, :, :], t1[:, :, :], wide(net.base128[:, :], 2, P), ALU.subtract))
                dve.sem_inc(net.dve_done.sem, 1)
                link(dve.tensor_scalar(t1[:, :, :], dloc[:, :, :], 0.0, None, ALU.is_ge))
                link(dve.scalar_tensor_tensor(out=inr[:, :, :], in0=dloc[:, :, :], scalar=float(P),
                                              in1=t1[:, :, :], op0=ALU.is_lt, op1=ALU.mult))
                link(dve.tensor_tensor(real[:, :, :], real[:, :, :], inr[:, :, :], ALU.mult))
                link(dve.scalar_tensor_tensor(out=flag[:, :, :], in0=flag[:, :, :], scalar=-BIG,
                                              in1=inr[:, :, :], op0=ALU.mult, op1=ALU.mult))
                link(dve.tensor_scalar(hole[:, :, :], inr[:, :, :], BIG, -BIG, ALU.mult, ALU.add))
                link(dve.tensor_scalar(t1[:, :, :], inr[:, :, :], -99.0, 99.0, ALU.mult, ALU.add))
                link(dve.tensor_tensor(styp[:, :, :], F["typ"][:, :, :], t1[:, :, :], ALU.add))
                link(dve.tensor_scalar(ri[:, :, :], VR[:, :, 0, :], P - 1, None, ALU.bitwise_and))
                link(dve.tensor_copy(t1[:, :, :], ri[:, :, :]))
                link(dve.scalar_tensor_tensor(out=t1[:, :, :], in0=t1[:, :, :], scalar=1.0,
                                              in1=real[:, :, :], op0=ALU.add, op1=ALU.mult))
                link(dve.tensor_scalar(F["slo"][:, :, :], t1[:, :, :], -1.0, None, ALU.add))
                link(dve.tensor_scalar(ri[:, :, :], VR[:, :, 0, :], 7, None, ALU.logical_shift_right))
                dve.tensor_copy(F["shi"][:, :, :], ri[:, :, :]).then_inc(net.dve_done.sem, 1)

            @block.scalar
            def _(act):
                for k, n in enumerate(names):
                    for h in range(2):
                        act.wait_ge(net.pe_done.sem, net.pe_done.after(2 * k + h + 1))
                        a = h * 512
                        b = min(S, a + 512)
                        act.copy(dest[n][:, a:b], pt[:, k % 2, h, 0:b - a]).then_inc(net.act_done.sem, 1)

            @block.tensor
            def _(pe):
                for k, n in enumerate(names):
                    if made[n]:
                        pe.wait_ge(net.dve_done.sem, net.dve_done.after(made[n]))
                    for h in range(2):
                        if k >= 2:
                            pe.wait_ge(net.act_done.sem, net.act_done.after(2 * (k - 2) + h + 1))
                        groups = range(4 * h, min(RG, 4 * h + 4))
                        for g in groups:
                            r = rows[g]
                            ins = pe.transpose(pt[:, k % 2, h, (g % 4) * P:(g % 4) * P + r], F[n][0:r, g, :],
                                               net.ident[0:r, 0:r])
                        ins.then_inc(net.pe_done.sem, 1)

            @block.sync
            def _(sp):
                sp.wait_ge(net.dve_done.sem, net.dve_done.after(3))
                for k, b in enumerate((flag, hole, styp)):
                    sp.dma_start(net.lin[k, 0:RG * P * P].rearrange("(g p q) -> p g q", p=P, q=P),
                                 b[:, :, :]).then_inc(net.stored.sem, 16)
                sp.wait_ge(net.stored.sem, net.stored.after(48))
                V = net.V
                sp.dma_start(net.seg[0:P - 1, :], bass.AP(tensor=net.lin.tensor, offset=0,
                                                          ap=[[S, P - 1], [1, S + 1]])).then_inc(net.loaded.sem, 16)
                sp.dma_start(net.seg[P - 1:P, 0:S], net.lin[0, V - S:V].rearrange("(p q) -> p q", p=1)
                             ).then_inc(net.loaded.sem, 16)
                sp.dma_start(net.seg[P - 1:P, S:S + 1], net.lin[0, V - 1:V].rearrange("(p q) -> p q", p=1)
                             ).then_inc(net.loaded.sem, 16)
                for k, b in ((1, net.hole), (2, net.styp)):
                    sp.dma_start(b[:, :], net.lin[k, 0:V].rearrange("(p q) -> p q", p=P)).then_inc(net.loaded.sem, 16)
                sp.wait_ge(net.loaded.sem, net.loaded.after(80))
    net.dve_done.passed(3)
    net.act_done.passed(2 * len(names))
    net.pe_done.passed(2 * len(names))
    net.stored.passed(48)
    net.loaded.passed(80)



def weight_loads(net, a):
    L = 2
    net.vec, off = {}, 0
    rows = [("bq0", a["L0_gnn_Wq_b"]), ("bias0", a["L0_gnn_bias"]), ("gamma0", a["L0_gnn_ln_gamma"]),
            ("beta0", a["L0_gnn_ln_beta"]), ("b_in", a["L3_gnn_b_in"])]
    for l in range(L):
        rows += [((n, l), a[f"L3_gnn_{n}"][l]) for n in ("bq", "bk", "bv", "bskip")]
        rows += [(("We", l), a["L3_gnn_We"][l, 0]), (("Wbeta", l), a["L3_gnn_Wbeta"][l].rearrange("f a -> (f a)")),
                 (("gamma", l), a["L3_gnn_bn_gamma"][l]), (("beta", l), a["L3_gnn_bn_beta"][l])]
    mats = [("Wq0", a["L0_gnn_Wq_w"])] + [(f"Wk{i + 1}", a["L0_gnn_Wk_w"][i * D:(i + 1) * D, :]) for i in range(3)]
    mats += [("W_in", a["L3_gnn_W_in"])]
    for l in range(L):
        mats += [((n, l), a[f"L3_gnn_{n}"][l]) for n in ("Wq", "Wk", "Wv", "Wskip")]
    net.mat = {}
    net.weights_all = 16 * (len(rows) + len(mats) + 2)

    def issue(act):
        nonlocal off
        for name, v in rows:
            n = v.shape[0]
            net.vec[name] = net.VB[:, off:off + n]
            act.dma_start(net.VB[:, off:off + n], v.rearrange("(a n) -> a n", a=1).to_broadcast([P, n])
                          ).then_inc(net.weights_sem, 16)
            off += n
        for k, (name, m) in enumerate(mats):
            net.mat[name] = net.WB[:, k * D:(k + 1) * D]
            act.dma_start(net.WB[:, k * D:(k + 1) * D], m).then_inc(net.weights_sem, 16)
        act.dma_start(net.kb_col[:, :], a["L0_gnn_Wk_b"].rearrange("(p a) -> p a", a=1)
                      ).then_inc(net.weights_sem, 16)
        act.dma_start(net.rule_i[:, :], a["L0_gnn_rule_ids"].rearrange("(p a) -> p a", a=1)
                      ).then_inc(net.weights_sem, 16)
    return issue



def inverse_root(net, stat, tmp):
    with net.nc.Block() as block:
        @block.scalar
        def _(act):
            act.sqrt(tmp, stat).then_inc(net.act_done.sem, 1)

        @block.vector
        def _(dve):
            link = net.dve.on(dve)
            dve.wait_ge(net.act_done.sem, net.act_done.after(1))
            link(dve.reciprocal(tmp, tmp))
            link(dve.tensor_tensor(stat, stat, tmp, ALU.mult))
            link(dve.tensor_tensor(stat, stat, tmp, ALU.mult))
            link(dve.tensor_scalar(stat, stat, -0.5, 1.5, ALU.mult, ALU.add))
            link(dve.tensor_tensor(stat, stat, tmp, ALU.mult))
    net.act_done.passed(1)


def centre_rows(dve, link, src, dst, tmp, st):
    link(dve.tensor_reduce(st[:, 0, :], src, AX, ALU.add))
    link(dve.tensor_scalar(st[:, 0, :], st[:, 0, :], -1.0 / D, None, ALU.mult))
    link(dve.tensor_tensor(tmp, src, wide(st[:, 0, :], 2, D), ALU.add))
    link(dve.tensor_tensor(dst, tmp, tmp, ALU.mult))
    link(dve.tensor_reduce(st[:, 1, :], dst, AX, ALU.add))
    link(dve.tensor_scalar(st[:, 1, :], st[:, 1, :], 1.0 / D, EPS, ALU.mult, ALU.add))


def centre(net, src, dst, tmp, st):
    by_vector(net, lambda dve, link: centre_rows(dve, link, src, dst, tmp, st))
    inverse_root(net, st[:, 1, :], st[:, 0, :])


def scale_relu(net, dst, tmp, st):
    by_vector(net, lambda dve, link: link(dve.scalar_tensor_tensor(
        out=dst, in0=tmp, scalar=0.0, in1=wide(st[:, 1, :], 2, D), op0=ALU.max, op1=ALU.mult)))


def norm_relu(net, src, dst, tmp, st):
    centre(net, src, dst, tmp, st)
    scale_relu(net, dst, tmp, st)


def turn_nodes(net, src, dst):
    NT = net.NT
    batches = [(b, min(NT, b + 4)) for b in range(0, NT, 4)]
    with ExitStack() as sc:
        pt = net.ps(sc, "turned", [P, 2, 512])
        with net.nc.Block() as block:
            @block.tensor
            def _(pe):
                for k, (a, b) in enumerate(batches):
                    if k >= 2:
                        pe.wait_ge(net.act_done.sem, net.act_done.after(k - 1))
                    for t in range(a, b):
                        ins = pe.transpose(pt[:, k % 2, (t - a) * P:(t - a + 1) * P], src[:, t, :], net.ident[:, :])
                    ins.then_inc(net.pe_done.sem, 1)

            @block.scalar
            def _(act):
                for k, (a, b) in enumerate(batches):
                    act.wait_ge(net.pe_done.sem, net.pe_done.after(k + 1))
                    act.copy(dst[:, a * P:b * P], pt[:, k % 2, 0:(b - a) * P]).then_inc(net.act_done.sem, 1)
    net.pe_done.passed(len(batches))
    net.act_done.passed(len(batches))


STORE_TILES = 5


def store_as_made(net, sp, table, rows, made):
    tiles = table.rearrange("(t p) d -> p t d", p=P)
    n = 0
    for a in range(0, net.NT, STORE_TILES):
        b = min(net.NT, a + STORE_TILES)
        sp.wait_ge(*made(b))
        sp.dma_start(tiles[:, a:b, :], rows[:, a:b, :]).then_inc(net.stored.sem, 16)
        n += 16
    sp.wait_ge(net.stored.sem, net.stored.after(n))
    return n


def scale_and_store(net, rows, scale, table):
    stored = 0
    with net.nc.Block() as block:
        @block.vector
        def _(dve):
            for k, a in enumerate(range(0, net.NT, STORE_TILES)):
                b = min(net.NT, a + STORE_TILES)
                dve.tensor_tensor(rows[:, a:b, :], rows[:, a:b, :], wide(scale[:, a:b], 2, D), ALU.mult
                                  ).then_inc(net.dve_done.sem, 1)

        @block.sync
        def _(sp):
            nonlocal stored
            stored = store_as_made(net, sp, table, rows, lambda t: (
                net.dve_done.sem, net.dve_done.after(ceil_div(t, STORE_TILES))))
    net.dve_done.passed(ceil_div(net.NT, STORE_TILES))
    net.stored.passed(stored)


def project(net, hT, w, n, parts, table=None, rows=None):
    stored = 0
    NT = net.NT
    with ExitStack() as sc:
        BANKS = 4
        pt = net.ps(sc, "rows", [P, BANKS, 512])
        with net.nc.Block() as block:
            @block.tensor
            def _(pe):
                for t in range(NT):
                    if t >= BANKS:
                        pe.wait_ge(net.dve_done.sem, net.dve_done.after(len(parts) * (t - BANKS + 1)))
                    pe.matmul(pt[:, t % BANKS, 0:n], hT[:, t * P:(t + 1) * P], w, start=True,
                              stop=True).then_inc(net.pe_done.sem, 1)

            @block.vector
            def _(dve):
                for t in range(NT):
                    dve.wait_ge(net.pe_done.sem, net.pe_done.after(t + 1))
                    for a, b, to, plus in parts:
                        if plus is None:
                            ins = dve.tensor_copy(to(t), pt[:, t % BANKS, a:b])
                        else:
                            ins = dve.tensor_tensor(to(t), pt[:, t % BANKS, a:b], plus, ALU.add)
                        ins.then_inc(net.dve_done.sem, 1)

            if table is not None:
                @block.sync
                def _(sp):
                    nonlocal stored
                    stored = store_as_made(net, sp, table, rows, lambda t: (
                        net.dve_done.sem, net.dve_done.after(t * len(parts))))
    net.pe_done.passed(NT)
    net.dve_done.passed(NT * len(parts))
    net.stored.passed(stored)


def rule_terms(net, a, BX):
    R, NR = net.R, net.NR
    with ExitStack() as sc:
        rel = net.sb(sc, "h_rel", [P, R])
        hr = net.sb(sc, "h_rule", [NR, D])
        hrT = net.sb(sc, "h_ruleT", [P, NR])
        pt = net.ps(sc, "rules", [P, 512])
        with net.nc.Block() as block:
            @block.sync
            def _(sp):
                sp.dma_start(net.WR[:, :, :], a["L0_gnn_W_r"].rearrange("r d o -> d r o")).then_inc(net.loaded.sem, 16)
                sp.wait_ge(net.weights_sem, net.weights_all)
                sp.wait_ge(net.loaded.sem, net.loaded.after(16))

            @block.gpsimd
            def _(pool):
                pool.wait_ge(net.weights_sem, net.weights_all)
                pool.indirect_dma_start(out=hr[:, :], out_offset=None, in_=a["L0_gnn_rule_emb"],
                                        in_offset=bass.IndirectOffsetOnAxis(ap=net.rule_i[:, 0:1], axis=0)
                                        ).then_inc(net.picked.sem, 16)
                pool.wait_ge(net.picked.sem, net.picked.after(16))

            @block.vector
            def _(dve):
                link = net.dve.on(dve)
                dve.wait_ge(net.loaded.sem, net.loaded.after(16))
                link(dve.tensor_reduce(rel[:, :], net.WR[:, :, :], AX, ALU.add))
                dve.tensor_scalar(rel[:, :], rel[:, :], 1.0 / D, None, ALU.mult).then_inc(net.dve_done.sem, 1)
                dve.wait_ge(net.pe_done.sem, net.pe_done.after(1))
                dve.tensor_copy(hrT[:, :], pt[:, 0:NR]).then_inc(net.dve_done.sem, 1)
                dve.wait_ge(net.pe_done.sem, net.pe_done.after(3))
                link(dve.tensor_scalar(BX[:, 0:R], pt[:, 0:R], net.kb_col[:, 0:1], None, ALU.add))
                link(dve.tensor_copy(BX[:, R:R + NR], pt[:, R:R + NR]))

            @block.tensor
            def _(pe):
                pe.wait_ge(net.picked.sem, net.picked.after(16))
                pe.transpose(pt[:, 0:NR], hr[:, :], net.ident[0:NR, 0:NR]).then_inc(net.pe_done.sem, 1)
                pe.wait_ge(net.weights_sem, net.weights_all)
                pe.wait_ge(net.dve_done.sem, net.dve_done.after(2))
                pe.matmul(pt[:, 0:R], net.mat["Wk2"], rel[:, :], start=True, stop=True).then_inc(net.pe_done.sem, 1)
                pe.matmul(pt[:, R:R + NR], net.mat["Wk3"], hrT[:, :], start=True,
                          stop=True).then_inc(net.pe_done.sem, 1)
    net.loaded.passed(16)
    net.picked.passed(16)
    net.dve_done.passed(2)
    net.pe_done.passed(3)



def gather_rows(net, pool, taken, slots, indices, table, gathered, spilled=None):
    stage = net.index_stage

    def copy_indices(i, place):
        pool.tensor_copy(stage[:, place, :], indices[:, bass.ds(i * IT, IT)]).then_inc(net.staged.sem, 1)

    def iteration(i, place, last=False):
        for g in range(groups_in(net, i)):
            n = i * NG + (g + 1)
            if g == 0:
                pool.wait_ge(net.staged.sem, net.staged.after(i + 1))
            pool.wait_ge(*taken(n))
            pool.sem_inc(net.pool_turn, 1)
            if spilled:
                pool.wait_ge(spilled.sem, spilled.after(n))
                pool.sem_inc(net.pool_turn, 1)
            if g == NG - 1 and not last:
                copy_indices(i + 1, 1 - place)
            for e in range(GS):
                k = g * GS + e
                pool.indirect_dma_start(out=slots[:, g, e, :], out_offset=None, in_=table,
                                        in_offset=bass.IndirectOffsetOnAxis(ap=stage[:, place, k:k + 1], axis=0)
                                        ).then_inc(gathered[g].sem, 16)

    copy_indices(0, 0)
    pairs = (net.ITERS - 1) // 2
    with pool.Fori(0, pairs) as j:
        iteration(2 * j, 0)
        iteration(2 * j + 1, 1)
    for i in range(2 * pairs, net.ITERS):
        iteration(i, i % 2, i == net.ITERS - 1)


def groups_in(net, i):
    return min(NG, net.GROUPS - i * NG) if isinstance(i, int) else NG


def each_group(net, eng, body, iters=None):
    def iteration(i):
        for g in range(groups_in(net, i)):
            body(i, g, i * NG + (g + 1), i * IT + g * GS)

    looped = min(iters or net.ITERS, net.GROUPS // NG)
    with eng.Fori(0, looped) as i:
        iteration(i)
    for i in range(looped, net.ITERS):
        iteration(i)


class StepTiles:

    def __init__(self, net, eng, name):
        self.net, self.eng = net, eng
        self.regs = [eng.alloc_register(f"loop{net.loops}_{name}{e}") for e in range(GS)]

    def at(self, col):
        self.eng.load(self.regs, self.net.tile_t[0:1, bass.ds(col, GS)])
        return [self.eng.snap(r, min_val=0, max_val=self.net.NT - 1) for r in self.regs]


def onehots(net, dve, OH, col, slot, steps=GS):
    return dve.tensor_tensor(OH[:, slot, 0:steps, :], wide(net.iota[:, :], 1, steps),
                             wide(net.dloc[:, bass.ds(col, steps)], 2, P), ALU.is_equal)


def score_pass(net, kind, table, heads, hT=None, proj=None, v_rows=None):
    nc, S, R, NT = net.nc, net.S, net.R, net.NT
    rel = kind == "rel"
    XC = (R + net.NR) if rel else heads
    with ExitStack() as sc:
        K = net.sb(sc, "k_rows", [P, NG, GS, table.shape[1]])
        OH = net.sb(sc, "onehot", [P, NG, GS, P])
        OT = net.sb(sc, "onehotT", [P, 2, GS, P])
        PR = net.sb(sc, "products", [P, GS, D])
        R1 = net.sb(sc, "sums", [P, GS, heads])
        net.index_stage = net.sb(sc, "index_stage", [P, 2, IT], I32)
        pT = [net.ps(sc, f"pT{b}", [P, GS, P]) for b in range(2)]
        pQX = [net.ps(sc, f"pQX{b}", [P, GS, 256]) for b in range(2)]
        gathered = net.gather_sems()
        sem = net.loop_sem
        onehot_ready, turned, copied = sem("onehot_ready"), sem("turned"), sem("turned_copied")
        if rel:
            TY = net.sb(sc, "onehot_type", [P, GS, R])
            TX = net.sb(sc, "type_terms", [P, GS, R])
            R2 = net.sb(sc, "type_sums", [P, GS])
            LO = net.sb(sc, "onehot_src_lo", [P, 2, GS, P])
            HI = net.sb(sc, "onehot_src_hi", [P, 2, GS, NT])
            HS = net.sb(sc, "h_tile", [P, P])
            PO = net.sb(sc, "proj_rows", [P, NG, 512])
            pP = net.ps(sc, "pP", [P, 512])
            pH = net.ps(sc, "pH", [P, 512])
            vec = Progress(sem("scored"), ["onehot_type", "product", "type_terms", "taken", "sum", "type_sum",
                                           "score"])
            src_ready = sem("src_onehot_ready")
            mm = Progress(sem("expanded"), ["expanded", "counted"])
            proj_made, proj_copied = sem("proj_made"), sem("proj_copied")
            tile_placed, proj_free = sem("h_tile_placed"), sem("proj_slot_free")
            proj_stored = [sem(f"proj_stored{g}") for g in range(NG)]
            per_tile = R * D // (512 * NG)
            PI = NT * per_tile
            projv = proj.rearrange("(n r) o -> n (r o)", r=R)
            WRf = net.WR[:, :, :].rearrange("p r o -> p (r o)")
        else:
            spilled = sem("v_slot_spilled")
            v_stored = [sem(f"v_stored{g}") for g in range(NG)]
            TX = net.sb(sc, "weight_terms", [P, GS, heads])
            vec = Progress(sem("scored"), ["product", "taken", "sum", "score"])
            mm = Progress(sem("expanded"), ["expanded"])
            PI = None

        def makes_proj(i):
            return rel and not (isinstance(i, int) and i >= PI)

        with nc.Block() as block:
            @block.gpsimd
            def _(pool):
                gather_rows(net, pool, lambda n: (vec.sem, vec.at(n - NG, "taken")), K, net.src_i, table, gathered,
                            None if rel else spilled)

            @block.tensor
            def _(pe):
                mm.credit(pe)
                tiles = StepTiles(net, pe, "tile")

                def turn(n, slot, b):
                    pe.wait_ge(onehot_ready.sem, onehot_ready.after(n))
                    for e in range(GS):
                        ins = pe.transpose(pT[b][:, e, :], OH[:, slot, e, :], net.ident[:, :])
                    ins.then_inc(turned.sem, 1)

                def body(i, g, n, col):
                    b = g % 2
                    if makes_proj(i):
                        pe.wait_ge(tile_placed.sem, tile_placed.after(i + 1))
                        pe.wait_ge(proj_copied.sem, proj_copied.after(n))
                        pe.matmul(pP[:, :], HS[:, :], WRf[:, bass.ds((i % per_tile) * (NG * 512) + g * 512, 512)],
                                  start=True, stop=True).then_inc(proj_made.sem, 1)
                    tile = tiles.at(col + GS)
                    pe.wait_ge(copied.sem, copied.after(n + 1))
                    pe.wait_ge(vec.sem, vec.at(n - 2, "taken"))
                    for e, t in enumerate(tile):
                        ins = pe.matmul(pQX[b][:, e, 0:D + XC], OT[:, b, e, :],
                                        net.QX[:, bass.ds(t, 1), 0:D + XC], start=True, stop=True)
                    ins.then_inc(*mm.did("expanded"))
                    turn(n + 1, (g + 1) % NG, 1 - b)
                    if rel:
                        pe.wait_ge(src_ready.sem, src_ready.after(n))
                        for e in range(GS):
                            ins = pe.matmul(pH[:, 0:NT], LO[:, b, e, :], HI[:, b, e, :], start=False,
                                            stop=False, skip_group_check=True)
                        ins.then_inc(*mm.did("counted"))

                if rel:
                    pe.sem_inc(proj_made.sem, 1)
                    pe.matmul(pH[:, 0:NT], net.zero[:, :], net.zero[:, 0:NT], start=True, stop=False,
                              skip_group_check=True)
                turn(1, 0, 0)
                each_group(net, pe, body, PI)
                if rel:
                    pe.matmul(pH[:, 0:NT], net.zero[:, :], net.zero[:, 0:NT], start=False, stop=True,
                              skip_group_check=True).then_inc(net.pe_done.sem, 1)

            @block.scalar
            def _(act):
                act.sem_inc(copied.sem, 1)
                if rel:
                    act.sem_inc(proj_copied.sem, 1)

                def body(i, g, n, col):
                    b = g % 2
                    if makes_proj(i) and g == 0:
                        act.wait_ge(proj_made.sem, proj_made.after(i * NG + 1))
                        act.sem_inc(net.act_turn, 1)
                        act.copy(HS[:, :], hT[:, bass.ds((i // per_tile) * P, P)]).then_inc(tile_placed.sem, 1)
                    act.wait_ge(turned.sem, turned.after(n))
                    act.wait_ge(mm.sem, mm.at(n - 2, "expanded"))
                    act.copy(OT[:, b, :, :], pT[b][:, :, :]).then_inc(copied.sem, 1)
                    if makes_proj(i):
                        act.wait_ge(proj_made.sem, proj_made.after(n + 1))
                        act.wait_ge(proj_free.sem, proj_free.after(n))
                        act.copy(PO[:, g, :], pP[:, :]).then_inc(proj_copied.sem, 1)

                each_group(net, act, body, PI)

            @block.sync
            def _(sp):
                if not rel:
                    sp.sem_inc(spilled.sem, NG)

                    def spill(i, g, n, col):
                        sp.wait_ge(gathered[g].sem, gathered[g].after(64 * i + 64))
                        sp.dma_start(v_rows[bass.ds((i * NG + g) * P, P), :].rearrange("p (e d) -> p e d", d=D),
                                     K[:, g, :, D:2 * D]).then_inc(v_stored[g].sem, 16)
                        sp.wait_ge(v_stored[g].sem, v_stored[g].after(16 * i + 16))
                        sp.sem_inc(spilled.sem, 1)

                    each_group(net, sp, spill)
                    return
                sp.sem_inc(proj_free.sem, NG)

                def body(i, g, n, col):
                    if not makes_proj(i):
                        return
                    sp.wait_ge(proj_copied.sem, proj_copied.after(n + 1))
                    sp.dma_start(projv[bass.ds((i // per_tile) * P, P),
                                       bass.ds((i % per_tile) * (NG * 512) + g * 512, 512)],
                                 PO[:, g, :]).then_inc(proj_stored[g].sem, 16)
                    sp.wait_ge(proj_stored[g].sem, proj_stored[g].after(16 * i + 16))
                    sp.sem_inc(proj_free.sem, 1)

                each_group(net, sp, body, PI)

            @block.vector
            def _(dve):
                vec.credit(dve)
                onehots(net, dve, OH, 0, 0).then_inc(onehot_ready.sem, 1)
                onehots(net, dve, OH, GS, 1).then_inc(onehot_ready.sem, 1)

                def src_onehots(cols, b):
                    dve.tensor_tensor(LO[:, b, :, :], wide(net.iota[:, :], 1, GS), wide(net.slo[:, cols], 2, P),
                                      ALU.is_equal)
                    dve.tensor_tensor(HI[:, b, :, :], wide(net.iota[:, 0:NT], 1, GS), wide(net.shi[:, cols], 2, NT),
                                      ALU.is_equal).then_inc(src_ready.sem, 1)

                if rel:
                    src_onehots(slice(0, GS), 0)

                def body(i, g, n, col):
                    b = g % 2
                    cols = bass.ds(col, GS)
                    px = pQX[b][:, :, D:D + XC]
                    dve.wait_ge(vec.sem, vec.at(n - 1, "score"))
                    if rel:
                        dve.tensor_tensor(TY[:, :, :], wide(net.iota[:, 0:R], 1, GS), wide(net.typ[:, cols], 2, R),
                                          ALU.is_equal).then_inc(*vec.did("onehot_type"))
                    dve.wait_ge(gathered[g].sem, gathered[g].after(64 * i + 64))
                    dve.wait_ge(mm.sem, mm.at(n, "expanded"))
                    dve.tensor_tensor(PR[:, :, :], K[:, g, :, 0:D], pQX[b][:, :, 0:D], ALU.mult
                                      ).then_inc(*vec.did("product"))
                    if rel:
                        dve.wait_ge(vec.sem, vec.at(n, "onehot_type"))
                        dve.tensor_tensor(TX[:, :, :], TY[:, :, :], px[:, :, 0:R], ALU.mult
                                          ).then_inc(*vec.did("type_terms"))
                        dve.tensor_copy(net.rule[:, cols, :], px[:, :, R:XC]).then_inc(*vec.did("taken"))
                        dve.wait_ge(vec.sem, vec.at(n, "type_terms"))
                        dve.tensor_reduce(R1[:, :, 0], PR[:, :, :], AX, ALU.add).then_inc(*vec.did("sum"))
                        dve.tensor_reduce(R2[:, :], TX[:, :, :], AX, ALU.add).then_inc(*vec.did("type_sum"))
                    else:
                        dve.tensor_tensor(TX[:, :, :], px, wide(net.w[:, cols], 2, heads), ALU.mult
                                          ).then_inc(*vec.did("taken"))
                        dve.wait_ge(vec.sem, vec.at(n, "product"))
                        dve.tensor_reduce(R1[:, :, :], PR[:, :, :].rearrange("p e (h c) -> p e h c", h=heads),
                                          AX, ALU.add).then_inc(*vec.did("sum"))
                    onehots(net, dve, OH, col + 2 * GS, (g + 2) % NG).then_inc(onehot_ready.sem, 1)
                    if rel:
                        dve.wait_ge(mm.sem, mm.at(n - 1, "counted"))
                        src_onehots(bass.ds(col + GS, GS), 1 - b)
                        dve.wait_ge(vec.sem, vec.at(n, "type_sum"))
                        dve.tensor_tensor(net.score[:, cols], R1[:, :, 0], R2[:, :], ALU.add
                                          ).then_inc(*vec.did("score"))
                    else:
                        dve.wait_ge(vec.sem, vec.at(n, "sum"))
                        dve.tensor_tensor(net.score[:, cols, :], R1[:, :, :], TX[:, :, :], ALU.add
                                          ).then_inc(*vec.did("score"))

                each_group(net, dve, body)
                if rel:
                    dve.wait_ge(net.pe_done.sem, net.pe_done.after(1))
                    dve.tensor_copy(net.hist[:, :], pH[:, 0:NT]).then_inc(net.dve.sem, 1)
                    net.dve.n += 1
                    dve.wait_ge(net.dve.sem, net.dve.n)
        if rel:
            net.pe_done.passed(1)


def sum_pass(net, kind, width, table=None, indices=None, heads=0, v_rows=None):
    nc, S, R, NT, NR = net.nc, net.S, net.R, net.NT, net.NR
    gathers, typed = table is not None, kind in ("mass", "rel")
    rows_in = 16 if v_rows is not None else 64
    with ExitStack() as sc:
        shared = kind in ("mass", "conv")
        own = GS // 2 if shared else GS
        sums_of = [0, 1, 2, 2] if shared else [0, 1, 0, 1]
        SUMS = max(sums_of) + 1
        acc = [net.acc] + [net.sb(sc, "more_sums", [P, NT, width]) for k in range(SUMS - 1)]
        OH = net.sb(sc, "onehot", [P, NG, GS, P])
        V = net.sb(sc, "rows", [P, NG, GS, D]) if kind != "mass" else None
        M = net.sb(sc, "summands", [P, 2, GS, width]) if kind != "plain" else None
        if typed:
            TY = net.sb(sc, "onehot_type", [P, GS, R])
        if kind == "rel":
            OT = net.sb(sc, "onehotT", [P, 2, GS, P])
            E4 = net.sb(sc, "typed_exp", [P, GS, R, NR])
            AT = net.sb(sc, "typed_share", [P, GS, R * NR])
            AV = net.sb(sc, "attention", [P, 2, GS])
            pT = [net.ps(sc, f"pT{b}", [P, GS, P]) for b in range(2)]
            pR = [net.ps(sc, f"pR{b}", [P, GS, R * NR]) for b in range(2)]
        net.index_stage = net.sb(sc, "index_stage", [P, 2, IT], I32)
        pA = [net.ps(sc, f"pA{b}", [P, 2, 512]) for b in range(2)]
        gathered = net.gather_sems()
        sem = net.loop_sem
        onehot_ready = sem("onehot_ready")
        if shared:
            away = net.sb(sc, "away", [P, 2, GS - own, P])
            onehot_act, act_steps, weights_in = sem("onehot_ready_act"), sem("distances"), sem("weights_in")
        adds = [f"add{e}" for e in range(own)]
        made = {"mass": ["onehot_type", "summands"], "rel": ["onehot_type", "typed_exp", "share", "attention"],
                "plain": [], "conv": ["summands"]}[kind]
        vec = Progress(sem("vector_summed"), made + adds)
        if shared:
            pooled = Progress(sem("pool_summed"), [f"add{e}" for e in range(own, GS)])
            handed = Progress(sem("products_copied"), ["products"])
            PC = net.sb(sc, "products_copy", [P, 2, GS - own, width])
        mm = Progress(sem("matrix_summed"), (["expanded"] if kind == "rel" else []) + ["aggregated"])
        if kind == "rel":
            rows = Progress(sem("rows_weighed"), ["rows"])
            turned, copied = sem("turned"), sem("turned_copied")
        with nc.Block() as block:
            @block.vector
            def _(dve):
                link = net.dve.on(dve)
                link(dve.memset(acc[0][:, :, :], 0.0))
                link(dve.memset(OH[:, NG - 1, :, :], 0.0))

            @block.gpsimd
            def _(pool):
                link = net.pool.on(pool)
                for a in acc[1:SUMS]:
                    link(pool.memset(a[:, :, :], 0.0))
                if M is not None:
                    link(pool.memset(M[:, 1, :, :], 0.0))
                if kind == "rel":
                    link(pool.memset(M[:, :, :, D:D + 1], 1.0))
                if V is not None:
                    link(pool.memset(V[:, NG - 1, :, :], 0.0))

        def add_steps(eng, progress, tile, steps, g, n, ready, products):
            b = (g - 1) % 2
            eng.wait_ge(*ready)
            for e in steps:
                to = acc[sums_of[e]][:, bass.ds(tile[e], 1), 0:width]
                before = [x for x in steps if x < e and sums_of[x] == sums_of[e]]
                if before:
                    eng.wait_ge(progress.sem, progress.at(n, f"add{before[-1]}"))
                elif e == steps[0]:
                    eng.wait_ge(progress.sem, progress.at(n - 1, f"add{steps[-1]}"))
                eng.tensor_tensor(to, to, products(b, e).unsqueeze(1), ALU.add).then_inc(*progress.did(f"add{e}"))

        with nc.Block() as block:
            if shared:
                @block.gpsimd
                def _(pool):
                    pooled.credit(pool)
                    tiles, steps = StepTiles(net, pool, "tile"), range(own, GS)

                    def add(i, g, n, col):
                        add_steps(pool, pooled, tiles.at(col), steps, g, n, (handed.sem, handed.at(n, "products")),
                                  lambda b, e: PC[:, b, e - own, :])

                    each_group(net, pool, add)
                    add(None, net.GROUPS % NG, net.GROUPS + 1, net.S)

            if gathers:
                @block.gpsimd
                def _(pool):
                    taken = {"rel": lambda n: (rows.sem, rows.at(n - NG, "rows")),
                             "plain": lambda n: (mm.sem, mm.at(n - NG + 1, "aggregated"))}[kind]
                    gather_rows(net, pool, taken, V, indices, table, gathered)

            if v_rows is not None:
                @block.sync
                def _(sp):
                    def load(i, g, n, col):
                        sp.wait_ge(vec.sem, vec.at(n - NG, "summands"))
                        sp.dma_start(V[:, g, :, :], v_rows[bass.ds((i * NG + g) * P, P), :].rearrange(
                            "p (e d) -> p e d", d=D)).then_inc(gathered[g].sem, 16)

                    each_group(net, sp, load)

            @block.tensor
            def _(pe):
                mm.credit(pe)
                tiles = StepTiles(net, pe, "tile")

                def turn(n, slot, b):
                    pe.wait_ge(onehot_ready.sem, onehot_ready.after(n))
                    for e in range(GS):
                        ins = pe.transpose(pT[b][:, e, :], OH[:, slot, e, :], net.ident[:, :])
                    ins.then_inc(turned.sem, 1)

                def aggregate(g, n):
                    s, b = (g - 1) % NG, (g - 1) % 2
                    pe.wait_ge(vec.sem, vec.at(n - 2, adds[-1]))
                    if shared:
                        pe.wait_ge(handed.sem, handed.at(n - 2, "products"))
                    if kind == "rel":
                        pe.wait_ge(rows.sem, rows.at(n - 1, "rows"))
                    elif made:
                        pe.wait_ge(vec.sem, vec.at(n - 1, made[-1]))
                    if kind == "conv":
                        pe.wait_ge(weights_in.sem, weights_in.after(n))
                    for e in range(GS):
                        row = M[:, b, e, :] if M is not None else V[:, s, e, :]
                        ins = pe.matmul(pA[b][:, e // 2, (e % 2) * 256:(e % 2) * 256 + width], OH[:, s, e, :],
                                        row, start=True, stop=True)
                    ins.then_inc(*mm.did("aggregated"))

                def body(i, g, n, col):
                    b = g % 2
                    if kind == "rel":
                        tile = tiles.at(col + GS)
                        pe.wait_ge(copied.sem, copied.after(n + 1))
                        pe.wait_ge(vec.sem, vec.at(n - 2, "share"))
                        for e, t in enumerate(tile):
                            ins = pe.matmul(pR[b][:, e, :], OT[:, b, e, :], net.QX[:, bass.ds(t, 1), 0:R * NR],
                                            start=True, stop=True)
                        ins.then_inc(*mm.did("expanded"))
                    else:
                        pe.wait_ge(onehot_ready.sem, onehot_ready.after(n))
                        if shared:
                            pe.wait_ge(onehot_act.sem, onehot_act.after(n))
                    if kind == "rel":
                        turn(n + 1, (g + 1) % NG, 1 - b)
                    aggregate(g, n)
                    if kind == "plain":
                        pe.wait_ge(gathered[g].sem, gathered[g].after(64 * i + 64))

                if kind == "rel":
                    turn(1, 0, 0)
                each_group(net, pe, body)
                if kind == "rel":
                    pe.wait_ge(mm.sem, mm.at(net.GROUPS, "aggregated"))
                    pe.sem_inc(*mm.did("expanded"))
                aggregate(net.GROUPS % NG, net.GROUPS + 1)

            @block.vector
            def _(dve):
                vec.credit(dve)
                tiles = StepTiles(net, dve, "tile")
                onehots(net, dve, OH, 0, 0, own).then_inc(onehot_ready.sem, 1)
                onehots(net, dve, OH, GS, 1, own).then_inc(onehot_ready.sem, 1)

                def add(tile, g, n):
                    add_steps(dve, vec, tile, range(own), g, n, (mm.sem, mm.at(n, "aggregated")),
                              lambda b, e: pA[b][:, e // 2, (e % 2) * 256:(e % 2) * 256 + width])

                def body(i, g, n, col):
                    b = g % 2
                    cols = bass.ds(col, GS)
                    if typed:
                        dve.wait_ge(vec.sem, vec.at(n - 1, made[1]))
                        dve.tensor_tensor(TY[:, :, :], wide(net.iota[:, 0:R], 1, GS), wide(net.typ[:, cols], 2, R),
                                          ALU.is_equal).then_inc(*vec.did("onehot_type"))
                    dve.wait_ge(mm.sem, mm.at(n - 1, "aggregated"))
                    onehots(net, dve, OH, col + 2 * GS, (g + 2) % NG, own).then_inc(onehot_ready.sem, 1)
                    if typed:
                        dve.wait_ge(vec.sem, vec.at(n, "onehot_type"))
                        to = M[:, b, :, :].rearrange("p e (r a) -> p e r a", a=NR) if kind == "mass" else E4[:, :, :, :]
                        dve.tensor_tensor(to, wide(TY[:, :, :], 3, NR), wide(net.rule[:, cols, :], 2, R), ALU.mult
                                          ).then_inc(*vec.did("summands" if kind == "mass" else "typed_exp"))
                    if kind == "rel":
                        tile = tiles.at(col)
                        dve.wait_ge(vec.sem, vec.at(n, "typed_exp"))
                        dve.wait_ge(mm.sem, mm.at(n, "expanded"))
                        dve.tensor_tensor(AT[:, :, :], pR[b][:, :, :], E4[:, :, :, :].rearrange("p e r a -> p e (r a)"),
                                          ALU.mult).then_inc(*vec.did("share"))
                        dve.wait_ge(rows.sem, rows.at(n - 2, "rows"))
                        dve.wait_ge(vec.sem, vec.at(n, "share"))
                        dve.tensor_reduce(AV[:, b, :], AT[:, :, :], AX, ALU.add).then_inc(*vec.did("attention"))
                    if kind == "conv":
                        dve.wait_ge(gathered[g].sem, gathered[g].after(rows_in * i + rows_in))
                        c = D // heads
                        dve.sem_inc(net.dve_turn, 1)
                        dve.tensor_tensor(M[:, b, :, 0:D].rearrange("p e (h c) -> p e h c", h=heads),
                                          V[:, g, :, :].rearrange("p e (h c) -> p e h c", h=heads),
                                          wide(net.score[:, cols, :], 3, c), ALU.mult).then_inc(*vec.did("summands"))
                    if kind != "rel":
                        tile = tiles.at(col)
                    add(tile, g, n)

                each_group(net, dve, body)
                if made:
                    dve.wait_ge(vec.sem, vec.at(net.GROUPS, adds[-1]))
                for m in made:
                    dve.sem_inc(*vec.did(m))
                add(tiles.at(net.S), net.GROUPS % NG, net.GROUPS + 1)
                dve.wait_ge(vec.sem, vec.at(net.GROUPS + 1, adds[-1]))
                if shared:
                    dve.wait_ge(pooled.sem, pooled.at(net.GROUPS + 1, f"add{GS - 1}"))
                link = net.dve.on(dve)
                for k in range(1, SUMS):
                    link(dve.tensor_tensor(acc[0][:, :, 0:width], acc[0][:, :, 0:width], acc[k][:, :, 0:width],
                                           ALU.add))

            if shared:
                @block.scalar
                def _(act):
                    def distances(col, slot, b, m):
                        for e in range(own, GS):
                            ins = act.activation(away[:, b, e - own, :], net.iota[:, :], ACT.Abs, scale=-1.0,
                                                 bias=net.dloc[:, bass.ds(col + e, 1)])
                        ins.then_inc(act_steps.sem, 1)
                        act.wait_ge(act_steps.sem, act_steps.after(m))
                        act.activation(OH[:, slot, own:GS, :], away[:, b, :, :], ACT.Relu, scale=-1.0,
                                       bias=net.ones[:, 0:1]).then_inc(onehot_act.sem, 1)

                    def hand_over(g, n):
                        b = (g - 1) % 2
                        act.wait_ge(pooled.sem, pooled.at(n - 2, f"add{GS - 1}"))
                        act.wait_ge(mm.sem, mm.at(n, "aggregated"))
                        act.copy(PC[:, b, :, :], pA[b][:, 1, :].rearrange("p (e c) -> p e c", c=256)[:, :, 0:width]
                                 ).then_inc(*handed.did("products"))

                    handed.credit(act)
                    distances(0, 0, 0, 1)
                    distances(GS, 1, 1, 2)

                    if kind == "conv":
                        act.sem_inc(weights_in.sem, 1)

                    def body(i, g, n, col):
                        b = g % 2
                        act.wait_ge(mm.sem, mm.at(n - 1, "aggregated"))
                        act.sem_inc(net.act_turn, 1)
                        if kind == "conv":
                            act.copy(M[:, b, :, D:D + 2 * heads], net.weights[:, bass.ds(col, GS), :]
                                     ).then_inc(weights_in.sem, 1)
                        distances(col + 2 * GS, (g + 2) % NG, g % 2, n + 2)
                        hand_over(g, n)

                    each_group(net, act, body)
                    hand_over(net.GROUPS % NG, net.GROUPS + 1)

            if kind == "rel":
                @block.scalar
                def _(act):
                    act.sem_inc(copied.sem, 1)
                    rows.credit(act)

                    def copy_turned(n, b):
                        act.wait_ge(turned.sem, turned.after(n))
                        act.wait_ge(mm.sem, mm.at(n - 2, "expanded"))
                        act.copy(OT[:, b, :, :], pT[b][:, :, :]).then_inc(copied.sem, 1)

                    copy_turned(1, 0)

                    def body(i, g, n, col):
                        b = g % 2
                        copy_turned(n + 1, 1 - b)
                        act.wait_ge(gathered[g].sem, gathered[g].after(64 * i + 64))
                        act.wait_ge(mm.sem, mm.at(n - 1, "aggregated"))
                        act.wait_ge(vec.sem, vec.at(n, "attention"))
                        for e in range(GS):
                            ins = act.activation(M[:, b, e, 0:D], V[:, g, e, :], ACT.Copy, scale=AV[:, b, e:e + 1])
                        ins.then_inc(*rows.did("rows"))

                    each_group(net, act, body)



def by_vector(net, work):
    with net.nc.Block() as block:
        @block.vector
        def _(dve):
            work(dve, net.dve.on(dve))


def row_groups(net):
    return [P] * (net.RG - 1) + [net.S - P * (net.RG - 1)]


def to_scan_layout(net, pairs):
    nc, RG, S, V = net.nc, net.RG, net.S, net.V
    full = (RG - 1) * P
    rest = S - full
    plane = net.plane_stored
    with ExitStack() as sc:
        RB = net.sb(sc, "rows_of_steps", [P, 2, RG, P])
        pt = [net.ps(sc, f"pt{k}", [P, 2, 512]) for k in range(2)]
        with nc.Block() as block:
            @block.tensor
            def _(pe):
                for k, (src, dst) in enumerate(pairs):
                    if k >= 2:
                        pe.wait_ge(net.act_done.sem, net.act_done.after(k - 1))
                    for g, r in enumerate(row_groups(net)):
                        ins = pe.transpose(pt[k % 2][0:r, g // 4, (g % 4) * P:(g % 4 + 1) * P],
                                           src[:, g * P:g * P + r], net.ident[:, :])
                    ins.then_inc(net.pe_done.sem, 1)

            @block.scalar
            def _(act):
                for k in range(len(pairs)):
                    act.wait_ge(net.pe_done.sem, net.pe_done.after(k + 1))
                    if k >= 2:
                        act.wait_ge(plane[k % 2].sem, plane[k % 2].after(32 * (k // 2)))
                    b = k % 2
                    act.copy(RB[:, b, 0:4, :], pt[b][:, 0, :].rearrange("p (g q) -> p g q", q=P))
                    act.copy(RB[:, b, 4:RG - 1, :], pt[b][:, 1, 0:(RG - 5) * P].rearrange("p (g q) -> p g q", q=P))
                    act.copy(RB[0:rest, b, RG - 1, :], pt[b][0:rest, 1, (RG - 5) * P:(RG - 4) * P]
                             ).then_inc(net.act_done.sem, 1)

            @block.sync
            def _(sp):
                for k, (src, dst) in enumerate(pairs):
                    sp.wait_ge(net.act_done.sem, net.act_done.after(k + 1))
                    sp.dma_start(net.lin[k, 0:full * P].rearrange("(g p q) -> p g q", p=P, q=P),
                                 RB[:, k % 2, 0:RG - 1, :]).then_inc(plane[k % 2].sem, 16)
                    sp.dma_start(net.lin[k, full * P:V].rearrange("(p q) -> p q", q=P),
                                 RB[0:rest, k % 2, RG - 1, :]).then_inc(plane[k % 2].sem, 16)
                for k in range(min(2, len(pairs))):
                    sp.wait_ge(plane[k].sem, plane[k].after(32 * ceil_div(len(pairs) - k, 2)))
                for k, (src, dst) in enumerate(pairs):
                    sp.dma_start(dst, net.lin[k, 0:V].rearrange("(p q) -> p q", p=P)).then_inc(net.loaded.sem, 16)
                sp.wait_ge(net.loaded.sem, net.loaded.after(16 * len(pairs)))
    net.pe_done.passed(len(pairs))
    net.act_done.passed(len(pairs))
    for k in range(2):
        plane[k].passed(32 * ceil_div(len(pairs) - k, 2))
    net.loaded.passed(16 * len(pairs))


def to_step_layout(net, pairs):
    nc, RG, S, V = net.nc, net.RG, net.S, net.V
    full = (RG - 1) * P
    rest = S - full
    with ExitStack() as sc:
        RB = net.sb(sc, "rows_of_steps", [P, 2, RG, P])
        pt = [net.ps(sc, f"pt{k}", [P, 2, 512]) for k in range(2)]
        with nc.Block() as block:
            @block.sync
            def _(sp):
                for k, (src, dst) in enumerate(pairs):
                    sp.dma_start(net.lin[k, 0:V].rearrange("(p q) -> p q", p=P), src).then_inc(net.stored.sem, 16)
                sp.wait_ge(net.stored.sem, net.stored.after(16 * len(pairs)))
                for k in range(len(pairs)):
                    if k >= 2:
                        sp.wait_ge(net.pe_done.sem, net.pe_done.after(k - 1))
                        sp.wait_ge(net.loaded.sem, net.loaded.after(32 * k))
                    sp.dma_start(RB[:, k % 2, 0:RG - 1, :],
                                 net.lin[k, 0:full * P].rearrange("(g p q) -> p g q", p=P, q=P)
                                 ).then_inc(net.loaded.sem, 16)
                    sp.dma_start(RB[0:rest, k % 2, RG - 1, :],
                                 net.lin[k, full * P:V].rearrange("(p q) -> p q", q=P)).then_inc(net.loaded.sem, 16)
                    if k % 2 == 0 and k + 1 < len(pairs):
                        sp.wait_ge(net.loaded.sem, net.loaded.after(32 * (k + 1)))

            @block.tensor
            def _(pe):
                for k in range(len(pairs)):
                    pe.wait_ge(net.loaded.sem, net.loaded.after(32 * (k + 1)))
                    if k >= 2:
                        pe.wait_ge(net.act_done.sem, net.act_done.after(k - 1))
                    for g, r in enumerate(row_groups(net)):
                        ins = pe.transpose(pt[k % 2][:, g // 4, (g % 4) * P:(g % 4) * P + r],
                                           RB[0:r, k % 2, g, :], net.ident[0:r, 0:r])
                    ins.then_inc(net.pe_done.sem, 1)

            @block.scalar
            def _(act):
                for k, (src, dst) in enumerate(pairs):
                    act.wait_ge(net.pe_done.sem, net.pe_done.after(k + 1))
                    act.copy(dst[:, 0:512], pt[k % 2][:, 0, :])
                    act.copy(dst[:, 512:S], pt[k % 2][:, 1, 0:S - 512]).then_inc(net.act_done.sem, 1)
    net.pe_done.passed(len(pairs))
    net.act_done.passed(len(pairs))
    net.stored.passed(16 * len(pairs))
    net.loaded.passed(32 * len(pairs))


class SegmentMax:

    def __init__(self, net, sc, channels):
        self.net, self.CH = net, channels
        self.start = net.sb(sc, "run_starts", [P, channels])
        self.first = net.sb(sc, "row_flags_right", [channels, P])
        self.second = net.sb(sc, "row_flags_left", [channels, P])
        self.carry = net.sb(sc, "row_states", [channels, P + 1])
        self.edge = net.sb(sc, "run_flags", [P, 2, channels])
        self.pt = net.ps(sc, "row_turned", [P, 512])
        self.pc = net.ps(sc, "run_turned", [P, 512])

    def flags(self):
        net, CH = self.net, self.CH
        with net.nc.Block() as block:
            @block.vector
            def _(dve):
                link = net.dve.on(dve)
                S = net.S
                for k in range(2):
                    link(dve.tensor_reduce(self.edge[:, k, 0:1], net.seg[:, k:k + S], AX, ALU.min))
                    dve.tensor_copy(self.edge[:, k, 1:CH], self.edge[:, k, 0:1].to_broadcast([P, CH - 1])
                                    ).then_inc(net.dve_done.sem, 1)
                for k, row in enumerate((self.first, self.second)):
                    dve.wait_ge(net.pe_done.sem, net.pe_done.after(k + 1))
                    link(dve.tensor_copy(row[:, :], (self.pt, self.pc)[k][0:CH, 0:P]))

            @block.tensor
            def _(pe):
                for k in range(2):
                    pe.wait_ge(net.dve_done.sem, net.dve_done.after(k + 1))
                    pe.transpose((self.pt, self.pc)[k][0:CH, 0:P], self.edge[:, k, :], net.ident[:, :]
                                 ).then_inc(net.pe_done.sem, 1)
        net.dve_done.passed(2)
        net.pe_done.passed(2)

    def vector(self, dve, link, X, Y, k=0):
        net, CH, S = self.net, self.CH, self.net.S
        right, left = net.seg[:, 0:S], net.seg[:, S:0:-1]
        done, turned = net.dve_done, net.pe_done

        def runs(to, flags, of, initial):
            for c in range(CH):
                ins = dve.tensor_tensor_scan(to(c), flags, of(c), initial(c), ALU.add, ALU.max)
            return ins

        def restart(n):
            dve.wait_ge(turned.sem, turned.after(4 * k + n))
            link(dve.tensor_copy(self.start[:, :], self.pc[:, 0:CH]))

        low = lambda c: -BIG
        begin = lambda c: self.start[:, c:c + 1]
        fy, fx = lambda c: Y[:, c, :], lambda c: X[:, c, :]
        by, bx = lambda c: Y[:, c, ::-1], lambda c: X[:, c, ::-1]
        runs(fy, right, fx, low).then_inc(done.sem, 1)
        link(dve.memset(self.carry[:, 0:1], -BIG))
        dve.wait_ge(turned.sem, turned.after(4 * k + 1))
        dve.tensor_tensor_scan(self.carry[:, 1:P + 1], self.first[:, :], self.pt[0:CH, 0:P], -BIG, ALU.add,
                               ALU.max).then_inc(done.sem, 1)
        restart(2)
        link(runs(fy, right, fx, begin))
        runs(bx, left, by, low).then_inc(done.sem, 1)
        link(dve.memset(self.carry[:, P:P + 1], -BIG))
        dve.wait_ge(turned.sem, turned.after(4 * k + 3))
        dve.tensor_tensor_scan(self.carry[:, P - 1::-1], self.second[:, ::-1], self.pt[0:CH, P - 1::-1], -BIG,
                               ALU.add, ALU.max).then_inc(done.sem, 1)
        restart(4)
        link(runs(bx, left, by, begin))

    def passed(self, uses):
        self.net.dve_done.passed(4 * uses)
        self.net.pe_done.passed(4 * uses)

    def tensor(self, pe, X, Y, k=0):
        net, CH, S = self.net, self.CH, self.net.S
        done, turned = net.dve_done, net.pe_done
        for j, (ends, of) in enumerate(((Y[:, :, S - 1], self.carry[:, 0:P]), (X[:, :, 0], self.carry[:, 1:P + 1]))):
            pe.wait_ge(done.sem, done.after(4 * k + 2 * j + 1))
            pe.transpose(self.pt[0:CH, 0:P], ends, net.ident[:, :]).then_inc(turned.sem, 1)
            pe.wait_ge(done.sem, done.after(4 * k + 2 * j + 2))
            pe.transpose(self.pc[:, 0:CH], of, net.ident[0:CH, 0:CH]).then_inc(turned.sem, 1)


def relation_weights(net):
    nc, S, R, NR = net.nc, net.S, net.R, net.NR
    scale = float(1.0 / D ** 0.5)
    CH = 4
    APART = 2.0 ** 100
    with ExitStack() as sc:
        X = net.sb(sc, "masked", [P, CH, S])
        Y = net.sb(sc, "scanned", [P, CH, S])
        A = [net.sb(sc, f"apart{k}", [P, CH, S]) for k in range(2)]
        SS = net.sb(sc, "scan_score", [P, S])
        TOP = net.sb(sc, "top", [P, CH, S])
        TM = net.sb(sc, "top_steps", [P, S])
        bias = net.sb(sc, "type_bias", [P, R])
        seg = SegmentMax(net, sc, CH)
        to_scan_layout(net, [(net.score[:, 0:S], SS[:, :])])
        seg.flags()

        def prepare(dve, link):
            link(dve.memset(TOP[:, :, :], -BIG))
            link(dve.tensor_scalar(bias[:, :], net.iota[:, 0:R], -APART, None, ALU.mult))
        by_vector(net, prepare)
        rounds = R // CH
        with nc.Block() as block:
            @block.scalar
            def _(act):
                for k in range(rounds):
                    if k >= 2:
                        act.wait_ge(net.dve_rounds.sem, net.dve_rounds.after(k - 1))
                    for c in range(CH):
                        r = k * CH + c
                        ins = act.activation(A[k % 2][:, c, :], net.styp[:, :], ACT.Abs, bias=bias[:, r:r + 1],
                                             scale=APART)
                    ins.then_inc(net.act_done.sem, 1)

            @block.tensor
            def _(pe):
                for k in range(rounds):
                    seg.tensor(pe, X, Y, k)

            @block.vector
            def _(dve):
                link = net.dve.on(dve)
                for k in range(rounds):
                    apart = A[k % 2][:, :, :]
                    dve.wait_ge(net.act_done.sem, net.act_done.after(k + 1))
                    link(dve.tensor_tensor(X[:, :, :], wide(SS[:, :], 1, CH), apart, ALU.subtract))
                    seg.vector(dve, link, X, Y, k)
                    dve.tensor_tensor(X[:, :, :], X[:, :, :], apart, ALU.subtract).then_inc(net.dve_rounds.sem, 1)
                    dve.wait_ge(net.dve_rounds.sem, net.dve_rounds.after(k + 1))
                    link(dve.tensor_tensor(TOP[:, :, :], TOP[:, :, :], X[:, :, :], ALU.max))
                for c in range(1, CH):
                    link(dve.tensor_tensor(TOP[:, 0, :], TOP[:, 0, :], TOP[:, c, :], ALU.max))
        net.act_done.passed(rounds)
        net.dve_rounds.passed(rounds)
        seg.passed(rounds)
        to_step_layout(net, [(TOP[:, 0, :], TM[:, :])])

        def shift(dve, link):
            xs = X[:, :, :].rearrange("p c s -> p (c s)").rearrange("p (s c) -> p s c", c=NR)
            rule = net.rule[:, 0:S, :]
            link(dve.tensor_tensor(xs, rule, wide(TM[:, :], 2, NR), ALU.add))
            link(dve.tensor_scalar(xs, xs, scale, None, ALU.mult))
            link(dve.tensor_tensor(rule, rule, wide(net.score[:, 0:S], 2, NR), ALU.add))
            link(dve.scalar_tensor_tensor(out=rule, in0=rule, scalar=scale, in1=xs, op0=ALU.mult, op1=ALU.subtract))
            link(dve.tensor_scalar(rule, rule, 0.0, None, ALU.min))
        by_vector(net, shift)
        exp_in_place(net, net.rule[:, 0:S, :])


def exp_in_place(net, ap, scale=1.0):
    with net.nc.Block() as block:
        @block.scalar
        def _(act):
            act.activation(ap, ap, ACT.Exp, scale=scale).then_inc(net.act_done.sem, 1)
            act.wait_ge(net.act_done.sem, net.act_done.after(1))
    net.act_done.passed(1)


def head_weights(net):
    nc, S, H = net.nc, net.S, net.HEADS
    scale = float(1.0 / (D // H) ** 0.5)
    with ExitStack() as sc:
        X = net.sb(sc, "head_scores", [P, H, S])
        Y = net.sb(sc, "scanned", [P, H, S])
        seg = SegmentMax(net, sc, H)
        score = net.score[:, 0:S, :]
        by_vector(net, lambda dve, link: link(dve.tensor_scalar(score, score, scale, None, ALU.mult)))
        to_scan_layout(net, [(net.score[:, 0:S, h], X[:, h, :]) for h in range(H)])
        seg.flags()
        with nc.Block() as block:
            @block.tensor
            def _(pe):
                seg.tensor(pe, X, Y)

            @block.vector
            def _(dve):
                link = net.dve.on(dve)
                link(dve.tensor_tensor(X[:, :, :], X[:, :, :], wide(net.hole[:, :], 1, H), ALU.add))
                seg.vector(dve, link, X, Y)
        seg.passed(1)
        top = Y[:, :, :].rearrange("p h s -> p (h s)").rearrange("p (s h) -> p s h", h=H)
        to_step_layout(net, [(X[:, h, :], top[:, :, h]) for h in range(H)])

        def shift(dve, link):
            link(dve.tensor_tensor(score, score, top, ALU.subtract))
            link(dve.tensor_scalar(score, score, 0.0, None, ALU.min))
        by_vector(net, shift)
        exp_in_place(net, score)
        by_vector(net, lambda dve, link: link(dve.tensor_tensor(
            net.wscore[:, 0:S, :], score, wide(net.w[:, 0:S], 2, H), ALU.mult)))


def build(nc, a, out):
    N, E, R = a["x"].shape[0], a["src"].shape[0], a["L0_gnn_W_r"].shape[0]
    with ExitStack() as ctx:
        net = Net(nc, ctx, N, E, R)
        NT, S, RG = net.NT, net.S, net.RG
        sb = lambda name, shape, dt=F32: net.sb(ctx, name, shape, dt)
        net.X = sb("X", [P, NT, D])
        net.ident = sb("ident", [P, P])
        net.ones = sb("ones", [P, P])
        net.iota = sb("iota", [P, P])
        net.tile_t = sb("tile_t", [1, GS + S], I32)
        net.src_i = sb("src_i", [P, net.SP], I32)
        net.pidx_i = sb("pidx_i", [P, net.SP], I32)
        net.dloc = sb("dloc", [P, net.SP])
        net.typ = sb("typ", [P, net.SP])
        net.w = sb("w", [P, net.SP])
        net.slo = sb("slo", [P, net.SP])
        net.shi = sb("shi", [P, net.SP])
        net.seg = sb("seg", [P, S + 1])
        net.hole = sb("hole", [P, S])
        net.styp = sb("styp", [P, S])
        net.NR = a["L0_gnn_rule_ids"].shape[0]
        net.VB = sb("weight_rows", [P, 3200])
        net.WB = sb("weight_mats", [P, 13 * D])
        net.kb_col = sb("kb_col", [P, 1])
        net.rule_i = sb("rule_i", [net.NR, 1], I32)
        net.zero = sb("zero", [P, P])
        net.hist = sb("hist", [P, NT])
        net.acc = sb("acc", [P, NT, W_ACC])
        net.QX = sb("QX", [P, NT, D + R + net.NR])
        net.H = sb("H", [P, NT, D])
        net.st = sb("stats", [P, 2, NT])
        net.chunks = net.dram("chunks", [RG * P, 5 * P], I32)
        net.tile_row = net.dram("tile_row", [RG * P], I32)
        net.lin = net.dram("lin", [4, RG * P * P])
        with ExitStack() as sc:
            net.CR = net.sb(sc, "CR", [P, RG, 5, P], I32)
            net.VR = net.sb(sc, "VR", [P, RG, 5, P], I32)
            net.iota_i = net.sb(sc, "iota_i", [P, P], I32)
            net.step_i = net.sb(sc, "step_i", [P, RG], I32)
            net.step_f = net.sb(sc, "step_f", [P, RG])
            net.chunk_i = net.sb(sc, "chunk_i", [P, RG], I32)
            net.base128 = net.sb(sc, "base128", [P, RG])
            weight = a["edge_weight1"].rearrange("e a -> (e a)").bitcast(I32)
            load_edges(net, a["src"], a["dst"], a["edge_type_32"], weight, a["x"], weight_loads(net, a))
            pair_steps(net)
            edge_fields(net)

        k_table = net.dram("k_table", [net.NP, D])
        proj = net.dram("proj_table", [net.NP * R, D])
        with ExitStack() as l0:
            net.rule = net.sb(l0, "rule_scores", [P, S + GS, net.NR])
            net.score = net.sb(l0, "scores", [P, S + GS])
            with ExitStack() as sc:
                net.WR = net.sb(sc, "W_r", [P, R, D])
                hT = net.sb(sc, "hT", [P, net.NP])
                with ExitStack() as sc2:
                    BX = net.sb(sc2, "BX", [P, R + net.NR])
                    KN = net.sb(sc2, "node_tmp", [P, NT, D])
                    rule_terms(net, a, BX)
                    inverse_root(net, net.st[:, 1, :], net.st[:, 0, :])
                    scale_relu(net, net.H[:, :, :], net.acc[:, :, 0:D], net.st)
                    turn_nodes(net, net.H, hT)
                    project(net, hT, net.WB[:, 0:2 * D], 2 * D, [
                        (0, D, lambda t: net.QX[:, t, 0:D], net.vec["bq0"]),
                        (D, 2 * D, lambda t: KN[:, t, :], None)], k_table, KN[:, :, :])
                    qT = KN[:, :, :].rearrange("p t d -> p (t d)")
                    turn_nodes(net, net.QX[:, :, 0:D], qT)
                    project(net, qT, BX[:, :], R + net.NR, [
                        (0, R + net.NR, lambda t: net.QX[:, t, D:D + R + net.NR], None)])
                score_pass(net, "rel", k_table, 1, hT, proj)
            relation_weights(net)
            sum_pass(net, "mass", R * net.NR)

            def inverse(dve, link):
                inv, mass = net.QX[:, :, 0:D], net.acc[:, :, 0:D]
                link(dve.tensor_scalar(mass, mass, 0.5, None, ALU.max))
                link(dve.reciprocal(inv, mass))
                link(dve.tensor_scalar(inv, inv, 1.0 / net.NR, None, ALU.mult))
            by_vector(net, inverse)
            sum_pass(net, "rel", D + 1, proj, net.pidx_i)

        in_deg = sb("in_degree", [P, NT])
        dis = sb("degree_roots", [P, NT])
        row = lambda v: wide(v, 1, NT)
        col = lambda s: wide(s, 2, D)
        acc, X, H, st = net.acc[:, :, 0:D], net.X[:, :, :], net.H[:, :, :], net.st

        with ExitStack() as sc:
            T = net.sb(sc, "node_tmp", [P, NT, D])

            def with_bias(dve, link):
                link(dve.tensor_copy(in_deg[:, :], net.acc[:, :, D]))
                link(dve.tensor_tensor(acc, acc, row(net.vec["bias0"]), ALU.add))
            by_vector(net, with_bias)
            centre(net, acc, H, T[:, :, :], st)

            def scale_add(dve, link):
                t = T[:, :, :]
                link(dve.tensor_tensor(t, t, col(st[:, 1, :]), ALU.mult))
                link(dve.tensor_tensor(t, t, row(net.vec["gamma0"]), ALU.mult))
                link(dve.tensor_tensor(t, t, row(net.vec["beta0"]), ALU.add))
                link(dve.tensor_scalar(t, t, 0.0, None, ALU.max))
                link(dve.tensor_tensor(X, X, t, ALU.add))
            by_vector(net, scale_add)

            table = net.dram("h_table", [net.NP, D])
            norm_relu(net, X, H, T[:, :, :], st)
            root = net.sb(sc, "root_tmp", [P, NT])
            by_vector(net, lambda dve, link: link(dve.tensor_scalar(dis[:, :], in_deg[:, :], 1.0, None, ALU.add)))
            inverse_root(net, dis[:, :], root[:, :])
            scale_and_store(net, H, dis[:, :], table)
        sum_pass(net, "plain", D, table, net.src_i)
        with ExitStack() as sc:
            T = net.sb(sc, "node_tmp", [P, NT, D])
            root = net.sb(sc, "root_tmp", [P, NT])
            by_vector(net, lambda dve, link: link(dve.tensor_scalar(dis[:, :], net.hist[:, :], 1.0, None, ALU.add)))
            inverse_root(net, dis[:, :], root[:, :])

            def residual(dve, link):
                link(dve.tensor_tensor(H, H, acc, ALU.add))
                link(dve.tensor_tensor(H, H, col(dis[:, :]), ALU.mult))
                link(dve.tensor_tensor(X, X, H, ALU.add))
            by_vector(net, residual)

            norm_relu(net, X, H, T[:, :, :], st)
            by_vector(net, lambda dve, link: link(dve.tensor_scalar(dis[:, :], net.hist[:, :], 1.0, None, ALU.max)))
            inverse_root(net, dis[:, :], root[:, :])
            scale_and_store(net, H, dis[:, :], table)
        sum_pass(net, "plain", D, table, net.src_i)

        net.HEADS = HD = 4
        kv_conv = net.dram("kv_conv", [net.NP, 2 * D])
        v_rows = net.dram("v_rows", [net.GROUPS * P, GS * D])
        XR = sb("skip", [P, NT, D])
        with ExitStack() as sc:
            T = net.sb(sc, "node_tmp", [P, NT, D])

            def residual2(dve, link):
                link(dve.tensor_tensor(acc, acc, col(dis[:, :]), ALU.mult))
                link(dve.tensor_tensor(X, X, acc, ALU.add))
            by_vector(net, residual2)

            norm_relu(net, X, T[:, :, :], H, st)
            hT = net.sb(sc, "hT", [P, net.NP])
            turn_nodes(net, T, hT)
            project(net, hT, net.mat["W_in"], D, [(0, D, lambda t: net.H[:, t, :], net.vec["b_in"])])
            by_vector(net, lambda dve, link: link(dve.tensor_scalar(H, H, 0.0, None, ALU.max)))

        for l in range(2):
            transformer_layer(net, l, XR, kv_conv, v_rows)

        by_vector(net, lambda dve, link: link(dve.tensor_tensor(X, X, H, ALU.add)))
        with nc.Block() as block:
            @block.sync
            def _(sp):
                full = (NT - 1) * P
                sp.dma_start(out[0:full, :].rearrange("(t p) d -> p t d", p=P), net.X[:, 0:NT - 1, :]
                             ).then_inc(net.stored.sem, 16)
                sp.dma_start(out[full:N, :], net.X[0:net.LAST, NT - 1, :]).then_inc(net.stored.sem, 16)
                sp.wait_ge(net.stored.sem, net.stored.after(32))


def transformer_layer(net, l, XR, kv_table, v_rows):
    nc, NT, HD = net.nc, net.NT, net.HEADS
    C = D // HD
    H, acc = net.H[:, :, :], net.acc[:, :, 0:D]
    row = lambda v: wide(v, 1, NT)
    col = lambda s: wide(s, 2, D)
    heads = lambda ap: ap.rearrange("p t (h c) -> p t h c", h=HD)
    We = net.vec[("We", l)]
    with ExitStack() as sc:
        KV = net.sb(sc, "kv_nodes", [P, NT, 2 * D])
        with ExitStack() as sc2:
            hT = net.sb(sc2, "hT", [P, net.NP])
            turn_nodes(net, net.H, hT)
            k = 5 + 4 * l
            project(net, hT, net.WB[:, k * D:(k + 4) * D], 4 * D, [
                (0, D, lambda t: net.QX[:, t, 0:D], net.vec[("bq", l)]),
                (D, 2 * D, lambda t: KV[:, t, 0:D], net.vec[("bk", l)]),
                (2 * D, 3 * D, lambda t: KV[:, t, D:2 * D], net.vec[("bv", l)]),
                (3 * D, 4 * D, lambda t: XR[:, t, :], net.vec[("bskip", l)])], kv_table, KV[:, :, :])

        def edge_term(dve, link):
            k = KV[:, :, 0:D]
            link(dve.tensor_tensor(k, net.QX[:, :, 0:D], row(We), ALU.mult))
            link(dve.tensor_reduce(net.QX[:, :, D:D + HD], heads(k), AX, ALU.add))
        by_vector(net, edge_term)
    with ExitStack() as sc:
        net.weights = net.sb(sc, "head_weights", [P, net.S, 2 * HD])
        net.score, net.wscore = net.weights[:, :, 0:HD], net.weights[:, :, HD:2 * HD]
        score_pass(net, "conv", kv_table, HD, v_rows=v_rows)
        head_weights(net)
        sum_pass(net, "conv", D + 2 * HD, heads=HD, v_rows=v_rows)
    with ExitStack() as sc:
        T = net.sb(sc, "node_tmp", [P, NT, D])
        U = net.sb(sc, "node_tmp2", [P, NT, D])
        z = net.sb(sc, "gate", [P, NT])
        inv = net.sb(sc, "mass_inverse", [P, NT, HD])
        t, u, xr = T[:, :, :], U[:, :, :], XR[:, :, :]
        Wb = net.vec[("Wbeta", l)]

        def gate_logit(dve, link):
            wide_c = lambda s: wide(s, 3, C)
            We_h = wide(We.rearrange("p (h c) -> p h c", h=HD), 1, NT)
            link(dve.tensor_tensor(heads(t), We_h, wide_c(net.acc[:, :, D + HD:D + 2 * HD]), ALU.mult))
            link(dve.tensor_tensor(acc, acc, t, ALU.add))
            link(dve.tensor_scalar(inv[:, :, :], net.acc[:, :, D:D + HD], 0.5, None, ALU.max))
            link(dve.reciprocal(inv[:, :, :], inv[:, :, :]))
            link(dve.tensor_tensor(heads(acc), heads(acc), wide_c(inv[:, :, :]), ALU.mult))
            link(dve.tensor_tensor(Wb[:, 0:D], Wb[:, 0:D], Wb[:, 2 * D:3 * D], ALU.add))
            link(dve.tensor_tensor(Wb[:, D:2 * D], Wb[:, D:2 * D], Wb[:, 2 * D:3 * D], ALU.subtract))
            link(dve.tensor_tensor(t, acc, row(Wb[:, 0:D]), ALU.mult))
            link(dve.tensor_tensor(u, xr, row(Wb[:, D:2 * D]), ALU.mult))
            link(dve.tensor_tensor(t, t, u, ALU.add))
            link(dve.tensor_reduce(z[:, :], t, AX, ALU.add))
            link(dve.tensor_scalar(z[:, :], z[:, :], -80.0, None, ALU.max))
        by_vector(net, gate_logit)
        exp_in_place(net, z[:, :], scale=-1.0)

        def gated(dve, link):
            link(dve.tensor_scalar(z[:, :], z[:, :], 1.0, None, ALU.add))
            link(dve.reciprocal(z[:, :], z[:, :]))
            link(dve.tensor_tensor(t, xr, col(z[:, :]), ALU.mult))
            link(dve.tensor_scalar(z[:, :], z[:, :], -1.0, 1.0, ALU.mult, ALU.add))
            link(dve.tensor_tensor(acc, acc, col(z[:, :]), ALU.mult))
            link(dve.tensor_tensor(t, t, acc, ALU.add))
        by_vector(net, gated)
        batch_norm(net, T, U, net.vec[("gamma", l)], net.vec[("beta", l)])

        def activate(dve, link):
            link(dve.tensor_scalar(t, t, 0.0, None, ALU.max))
            link(dve.tensor_tensor(H, H, t, ALU.add))
        by_vector(net, activate)


def batch_norm(net, T, U, gamma, beta):
    NT, LAST = net.NT, net.LAST
    t, u = T[:, :, :], U[:, :, :]
    row = lambda v: wide(v, 1, NT)
    with ExitStack() as sc:
        mu = net.sb(sc, "mean", [P, D])
        var = net.sb(sc, "variance", [P, D])
        tmp = net.sb(sc, "root_tmp", [P, D])
        ps = net.ps(sc, "node_sums", [P, 2, 512])

        def sums(pe, src, k):
            for i in range(NT):
                n = P if i < NT - 1 else LAST
                ins = pe.matmul(ps[:, k, 0:D], net.ones[0:n, :], src[0:n, i, :], start=i == 0, stop=i == NT - 1)
            ins.then_inc(net.pe_done.sem, 1)

        with net.nc.Block() as block:
            @block.tensor
            def _(pe):
                sums(pe, T, 0)
                pe.wait_ge(net.dve_done.sem, net.dve_done.after(1))
                sums(pe, U, 1)

            @block.vector
            def _(dve):
                link = net.dve.on(dve)
                dve.wait_ge(net.pe_done.sem, net.pe_done.after(1))
                link(dve.tensor_scalar(mu[:, :], ps[:, 0, 0:D], 1.0 / net.N, None, ALU.mult))
                link(dve.tensor_tensor(t, t, row(mu[:, :]), ALU.subtract))
                dve.tensor_tensor(u, t, t, ALU.mult).then_inc(net.dve_done.sem, 1)
                dve.wait_ge(net.pe_done.sem, net.pe_done.after(2))
                link(dve.tensor_scalar(var[:, :], ps[:, 1, 0:D], 1.0 / net.N, EPS, ALU.mult, ALU.add))
        net.pe_done.passed(2)
        net.dve_done.passed(1)
        inverse_root(net, var[:, :], tmp[:, :])

        def scale(dve, link):
            link(dve.tensor_tensor(var[:, :], var[:, :], gamma, ALU.mult))
            link(dve.tensor_tensor(t, t, row(var[:, :]), ALU.mult))
            link(dve.tensor_tensor(t, t, row(beta), ALU.add))
        by_vector(net, scale)


def kernel(**inputs):
    import numpy as _np
    import concourse.bacc as _bacc
    from concourse import mybir as _mybir
    from concourse.bass_utils import run_bass_kernel_spmd as _run

    nc = _bacc.Bacc("TRN2", target_bir_lowering=False, num_devices=1)
    arrays, args = {}, {}
    for name, value in inputs.items():
        v = _np.ascontiguousarray(value)
        arrays[f"in_{name}"] = v
        args[name] = nc.dram_tensor(f"in_{name}", v.shape, _mybir.dt.from_np(v.dtype), kind="ExternalInput").ap()
    x = arrays["in_x"]
    out = nc.dram_tensor("out", x.shape, _mybir.dt.from_np(x.dtype), kind="ExternalOutput").ap()
    build(nc, args, out)
    r = _run(nc, [arrays], core_ids=[0])
    return r.results[0]["out"]
```
